# Optimizing a Trainium2 kernel written in Bass

```python
import numpy as np
import jax
import jax.numpy as jnp

def _softmax(x, axis=-1):
    return jax.nn.softmax(x, axis=axis)

def _gelu(x):
    return jax.nn.gelu(x, approximate=True)

def _silu(x):
    return jax.nn.silu(x)

def _sigmoid(x):
    return jax.nn.sigmoid(x)

def _layernorm(x, axis=-1, eps=1e-05):
    m = jnp.mean(x, axis=axis, keepdims=True)
    v = jnp.var(x, axis=axis, keepdims=True)
    return (x - m) / jnp.sqrt(v + eps)

def _scatter_add(tgt, idx, src, axis=0):
    return tgt.at[idx].add(src)

def _segment_sum(src, seg, n):
    return jax.ops.segment_sum(src, seg, n)
kernel_name = 'mk_gnn_ffn_d1_gnn_r16_b48b6b'

def setup_inputs(seed: int=0):
    np.random.seed(seed)
    _w = jnp.asarray

    def _rec_inputs():
        import jax
        import jax.numpy as jnp
        _gk = jax.random.key(seed)
        x = -0.0003713 + 1 * jax.random.normal(jax.random.fold_in(_gk, 1), (3125, 256), jnp.float32)
        _s = jax.random.randint(jax.random.fold_in(_gk, 2), (25000,), 0, 3125, jnp.int32)
        _d = jax.random.randint(jax.random.fold_in(_gk, 3), (25000,), 0, 3125, jnp.int32)
        _loop = jnp.arange(3125, dtype=jnp.int32)
        src = jnp.concatenate([_s, _d, _loop])
        dst = jnp.concatenate([_d, _s, _loop])
        _o = jnp.argsort(dst, stable=True)
        src = src[_o]
        dst = dst[_o]
        edge_attr_256 = -2.25437e-05 + 0.999858 * jax.random.normal(jax.random.fold_in(_gk, 11), (53125, 256), jnp.float32)
        return (x, src, dst, edge_attr_256)
    x, src, dst, edge_attr_256 = _rec_inputs()

    def _L0_gnn_setup():
        import jax, jax.numpy as jnp
        import numpy as np
        N_NODES = 3125
        N_EDGES = 15625
        EMBED_DIM = 256
        LEAKY_SLOPE = 0.01
        LN_EPS = 1e-05

        def _calc_messages(H, E, idx, W, b):
            Hh = H[idx]
            raw = jnp.concatenate([Hh, E, Hh + E, Hh * E], axis=1)
            return raw @ W.T + b
        key = jax.random.key(seed)
        ks = jax.random.split(key, 6)
        d = EMBED_DIM
        H = jax.random.normal(ks[0], (N_NODES, d), dtype=jnp.float32)
        E = jax.random.normal(ks[1], (N_EDGES, d), dtype=jnp.float32)
        ht = jax.random.randint(ks[2], (N_EDGES, 2), 0, N_NODES, dtype=jnp.int32)
        scale = 1.0 / np.sqrt(4 * d)
        W_fwd = jax.random.normal(ks[3], (d, 4 * d), dtype=jnp.float32) * scale
        W_back = jax.random.normal(ks[4], (d, 4 * d), dtype=jnp.float32) * scale
        b_fwd = jnp.zeros((d,), dtype=jnp.float32)
        b_back = jnp.zeros((d,), dtype=jnp.float32)
        gamma = jnp.ones((d,), dtype=jnp.float32)
        beta = jnp.zeros((d,), dtype=jnp.float32)
        return {'H': H, 'E': E, 'ht': ht, 'W_fwd': W_fwd, 'b_fwd': b_fwd, 'W_back': W_back, 'b_back': b_back, 'gamma': gamma, 'beta': beta}
    _L0_gnn_all = _L0_gnn_setup()
    _L0_gnn_in = {k: v for k, v in _L0_gnn_all.items() if k in ('W_fwd', 'b_fwd', 'W_back', 'b_back', 'gamma', 'beta')}
    del _L0_gnn_all

    def _L0_ffn_setup():
        import jax, jax.numpy as jnp
        import numpy as np
        B, K, D = (512, 16, 256)
        E = 32
        H = int(D * 0.25)
        key = jax.random.key(seed)
        ks = jax.random.split(key, 7)
        d_rs = D ** (-0.5)
        h_rs = H ** (-0.5)
        x = jax.random.normal(ks[0], (B, K, D), dtype=jnp.float32)
        router_w = jax.random.uniform(ks[1], (E, D), jnp.float32, -d_rs, d_rs)
        router_b = jax.random.uniform(ks[2], (E,), jnp.float32, -d_rs, d_rs)
        W1 = jax.random.uniform(ks[3], (E, D, H), jnp.float32, -h_rs, h_rs)
        b1 = jax.random.uniform(ks[4], (E, H), jnp.float32, -h_rs, h_rs)
        W2 = jax.random.uniform(ks[5], (E, H, D), jnp.float32, -d_rs, d_rs)
        b2 = jax.random.uniform(ks[6], (E, D), jnp.float32, -d_rs, d_rs)
        return {'x': x, 'router_w': router_w, 'router_b': router_b, 'W1': W1, 'b1': b1, 'W2': W2, 'b2': b2}
    _L0_ffn_all = _L0_ffn_setup()
    _L0_ffn_in = {k: v for k, v in _L0_ffn_all.items() if k in ('router_w', 'router_b', 'W1', 'b1', 'W2', 'b2')}
    del _L0_ffn_all
    return {'x': x, 'src': src, 'dst': dst, 'edge_attr_256': edge_attr_256, 'L0_gnn_W_fwd': _L0_gnn_in['W_fwd'], 'L0_gnn_b_fwd': _L0_gnn_in['b_fwd'], 'L0_gnn_W_back': _L0_gnn_in['W_back'], 'L0_gnn_b_back': _L0_gnn_in['b_back'], 'L0_gnn_gamma': _L0_gnn_in['gamma'], 'L0_gnn_beta': _L0_gnn_in['beta'], 'L0_ffn_router_w': _L0_ffn_in['router_w'], 'L0_ffn_router_b': _L0_ffn_in['router_b'], 'L0_ffn_W1': _L0_ffn_in['W1'], 'L0_ffn_b1': _L0_ffn_in['b1'], 'L0_ffn_W2': _L0_ffn_in['W2'], 'L0_ffn_b2': _L0_ffn_in['b2']}

def reference(x, src, dst, edge_attr_256, L0_gnn_W_fwd, L0_gnn_b_fwd, L0_gnn_W_back, L0_gnn_b_back, L0_gnn_gamma, L0_gnn_beta, L0_ffn_router_w, L0_ffn_router_b, L0_ffn_W1, L0_ffn_b1, L0_ffn_W2, L0_ffn_b2):
    import jax
    import jax.numpy as jnp

    def _L0_gnn_ref(H, E, ht, W_fwd, b_fwd, W_back, b_back, gamma, beta):
        import jax, jax.numpy as jnp
        import numpy as np
        N_NODES = 3125
        N_EDGES = 15625
        EMBED_DIM = 256
        LEAKY_SLOPE = 0.01
        LN_EPS = 1e-05

        def _calc_messages(H, E, idx, W, b):
            Hh = H[idx]
            raw = jnp.concatenate([Hh, E, Hh + E, Hh * E], axis=1)
            return raw @ W.T + b
        n = H.shape[0]
        heads = ht[:, 0]
        tails = ht[:, 1]
        messages_fwd = _calc_messages(H, E, heads, W_fwd, b_fwd)
        messages_back = _calc_messages(H, E, tails, W_back, b_back)
        msg_dst = jnp.concatenate([tails, heads])
        messages = jnp.concatenate([messages_fwd, messages_back], axis=0)
        agg = jax.ops.segment_sum(messages, msg_dst, num_segments=n)
        cnt = jax.ops.segment_sum(jnp.ones((messages.shape[0],), dtype=messages.dtype), msg_dst, num_segments=n)
        agg = agg / jnp.maximum(cnt, 1.0)[:, None]
        x = jax.nn.leaky_relu(agg, LEAKY_SLOPE) + H
        mu = jnp.mean(x, axis=-1, keepdims=True)
        var = jnp.var(x, axis=-1, keepdims=True)
        out = (x - mu) * jax.lax.rsqrt(var + LN_EPS) * gamma + beta
        return out

    def _L0_ffn_ref(x, router_w, router_b, W1, b1, W2, b2):
        import jax, jax.numpy as jnp
        import numpy as np
        B, K, D = (512, 16, 256)
        E = 32
        H = int(D * 0.25)
        xf = x.reshape(-1, D)
        logits = xf @ router_w.T + router_b
        idx = jnp.argmax(logits, axis=-1)
        w1t = jnp.take(W1, idx, axis=0)
        h = jnp.einsum('nd,ndh->nh', xf, w1t) + jnp.take(b1, idx, axis=0)
        h = jax.nn.relu(h)
        w2t = jnp.take(W2, idx, axis=0)
        out = jnp.einsum('nh,nhd->nd', h, w2t) + jnp.take(b2, idx, axis=0)
        out = jax.nn.relu(out)
        return out.reshape(x.shape)
    edge_index_t = jnp.stack([src, dst], axis=1)
    x = x + _L0_gnn_ref(_layernorm(x, axis=-1), edge_attr_256, edge_index_t, L0_gnn_W_fwd, L0_gnn_b_fwd, L0_gnn_W_back, L0_gnn_b_back, L0_gnn_gamma, L0_gnn_beta)
    x = x + _L0_ffn_ref(_layernorm(x, axis=-1)[None], L0_ffn_router_w, L0_ffn_router_b, L0_ffn_W1, L0_ffn_b1, L0_ffn_W2, L0_ffn_b2)[0]
    return x

_drawn_inputs = setup_inputs


def setup_inputs(seed=0):
    import zlib

    import numpy as np

    out = dict(_drawn_inputs(seed))
    spreads = {'L0_gnn_b_fwd': (0.0, 0.376),
     'L0_gnn_b_back': (0.0, 0.339),
     'L0_gnn_gamma': (1.0, 0.2),
     'L0_gnn_beta': (0.0, 0.1)}
    factors = {'L0_ffn_b1': 8.0, 'L0_ffn_b2': 4.555}
    for name, (base, spread) in spreads.items():
        noise = np.random.default_rng([zlib.crc32(name.encode()), seed]).standard_normal(out[name].shape)
        drawn = base * np.exp(spread * noise) if base else spread * noise
        out[name] = jnp.asarray(drawn.astype(out[name].dtype))
    for name, factor in factors.items():
        out[name] = (out[name] * factor).astype(out[name].dtype)
    return out
```

```python
import concourse.bass as bass
from concourse import mybir
from contextlib import ExitStack

F32, I32, U16, BF16 = mybir.dt.float32, mybir.dt.int32, mybir.dt.uint16, mybir.dt.bfloat16
ALU = mybir.AluOpType
ACT = mybir.ActivationFunctionType
AX = mybir.AxisListType

P = 128
N, D = 3125, 256
E = 53125
RP, RC = 125, 425
NBLK = (N + P - 1) // P
TAIL = N - (NBLK - 1) * P
UNROLL = 4
TILES = -(-((E + P - 1) // P + NBLK) // UNROLL) * UNROLL
GROUPS = TILES // UNROLL
SW = 3 * D + 1
SB = 2 * SW
NX, NH, SLOPE, EPS = 32, 64, 0.01, 1e-5
UC = NX * NH // P
NEVER = -1.0e30
TO, FROM = 0, 1


def gnn_ffn(nc, x, src, dst, edge, w_fwd, b_fwd, w_back, b_back, gamma, beta,
            router_w, router_b, w1, b1, w2, b2, out):
    assert RP * RC == E
    ctx = ExitStack()
    with ctx:
        def sb(name, cols, dt=F32, rows=P):
            return ctx.enter_context(nc.sbuf_tensor(name, [rows, cols], dt))

        def sem(name):
            return ctx.enter_context(nc.semaphore(name))

        h_dram = nc.dram_tensor("h_rows", (NBLK * P, D), F32, kind="Internal").ap()
        t_dram = nc.dram_tensor("tile_table", (P * TILES * 2, 3), I32, kind="Internal").ap()

        arena = sb("arena", NBLK * SB)
        at = [0]

        def carve(cols, dt=F32):
            words = cols if dt in (F32, I32) else (cols + 1) // 2
            a = at[0]
            at[0] = a + words
            assert at[0] <= NBLK * SB
            v = arena[:, a:a + words]
            return v if dt == F32 else v.bitcast(dt)

        x_sb = carve(NBLK * D)
        h_sb = carve(NBLK * D)
        keys = carve(2 * RC, I32)
        blk_i = carve(2 * RC, I32)
        low_i = carve(2 * RC, I32)
        blk_h = carve(2 * RC, BF16)
        ones_r = carve(RC)
        rank = carve(2 * RC)
        pos = carve(2 * RC)
        pos_i = carve(2 * RC, I32)
        row_i = carve(2 * RC, I32)
        col_i = carve(2 * RC, I32)
        row_id = carve(2 * RC, I32)
        member = carve(2 * NBLK * RC, U16)
        meta = carve(2 * RC * 3, I32)
        tile_n = carve(TILES)
        tile_blk = carve(2 * TILES)[0:1, :]
        S = arena[:, :].rearrange("p (b w) -> p b w", b=NBLK)

        w_gnn = sb("w_gnn", 2 * 6 * D)
        table = sb("table", TILES * 2 * 3, I32)
        X = sb("X", 2 * UNROLL * 2 * D)
        PROH = sb("PROH", 2 * 2 * (D + 1) + 2 * 2 * P)
        PR = PROH[:, 0:2 * 2 * (D + 1)]
        OH = PROH[:, 2 * 2 * (D + 1):]
        stage = PROH[:, 0:SB]
        idx = sb("idx", 2 * 2 * 2 * 2, I32)
        iota_f = sb("iota_f", P)
        ident = sb("ident", P)
        before = sb("before", P)
        ones_m = sb("ones_m", P)
        small = sb("small", 24 * 2 * NBLK)
        tile_blk_i = sb("tile_blk_i", 2 * TILES, I32, 1)
        t_init = table[:, :]
        w_raw = X[:, 0:2 * 2 * 4 * D]
        Xv = X[:, :].rearrange("p (d u w) -> p d u w", d=2, u=UNROLL)
        PRv = PR.rearrange("p (d u w) -> p d u w", d=2, u=2)
        OHv = OH.rearrange("p (d u w) -> p d u w", d=2, u=2)
        IDv = idx[:, :].rearrange("p (h u d f) -> p h u d f", h=2, u=2, d=2)

        def sm(i, cols=2 * NBLK, dt=F32):
            v = small[:, i * 2 * NBLK:i * 2 * NBLK + cols]
            return v if dt == F32 else v.bitcast(dt)

        ST = X[:, 0:2 * 6 * P].rearrange("p (d k n) -> p d k n", d=2, k=6)
        post = X[:, 2 * 6 * P:2 * 6 * P + 2 * D]
        v_a, v_h = post[:, 0:D], post[:, D:2 * D]
        rows = table[:, :].bitcast(F32)
        bf_r, bb_r, ga_r, be_r = (rows[:, i * D:(i + 1) * D] for i in range(4))
        rb_r = rows[:, 4 * D:4 * D + NX]
        xin = rows[:, 5 * D:6 * D]
        rw_raw = rows[0:NX, 6 * D:7 * D]
        rwT = rows[:, 7 * D:7 * D + 2 * NX]
        b2_s = rows[0:NX, 8 * D:9 * D]
        b1_b = w_gnn[0:NX, 0:NX * NH]
        xT = X[:, 0:2 * P]
        hid = X[:, 2 * P:2 * P + UC * P]
        xn_c = X[:, 2 * P + UC * P:2 * P + UC * P + D]
        ff_o = PR[:, 0:D]
        lg = OH[:, 0:NX]
        oh = OH[:, NX:2 * NX]
        ohT = OH[0:NX, P:2 * P]
        mx8 = OH[:, 2 * P:2 * P + 8]
        mi8 = OH[:, 2 * P + 8:2 * P + 16].bitcast(mybir.dt.uint32)
        mif = OH[:, 2 * P + 16:2 * P + 17]

        ps = [ctx.enter_context(nc.psum_tensor(f"ps{i}", [P, 1024], F32)) for i in range(4)]

        x_in = sem("x_in")
        keys_in = sem("keys_in")
        w_in = sem("w_in")
        const_ready = sem("const_ready")
        meta_id = sem("meta_id")
        v_step = sem("v_step")
        std_ready = sem("std_ready")
        var_ready = sem("var_ready")
        h_ready = sem("h_ready")
        h_out = sem("h_out")
        tinit_ready = sem("tinit_ready")
        tinit_out = sem("tinit_out")
        counts_ready = sem("counts_ready")
        base_ready = sem("base_ready")
        pos_ready = sem("pos_ready")
        meta_out = sem("meta_out")
        table_in = sem("table_in")
        blk_ready = sem("blk_ready")
        wsum_ready = sem("wsum_ready")
        wt_ready = sem("wt_ready")
        wt_read = sem("wt_read")
        cmp_done = sem("cmp_done")
        scan_done = [sem(f"scan_done{d}") for d in range(2)]
        rank_masked = [sem(f"rank_masked{d}") for d in range(2)]
        pick_done = [sem(f"pick_done{d}") for d in range(2)]
        own = [sem(f"own{i}") for i in range(6)]
        tb_done = sem("tb_done")
        sums_zero = sem("sums_zero")
        idx_first = sem("idx_first")
        idx_ready = [sem(f"idx_ready{h}") for h in range(2)]
        got = [[sem(f"got_{d}_{u}") for u in range(UNROLL)] for d in range(2)]
        rhs_ready = [[sem(f"rhs_ready_{d}_{u}") for u in range(UNROLL)] for d in range(2)]
        mm_done = [[sem(f"mm_done_{d}_{u}") for u in range(UNROLL)] for d in range(2)]
        summed = [sem(f"summed_{d}") for d in range(2)]
        loop_done = sem("loop_done")
        rows_in = sem("rows_in")
        sT_ready = [sem(f"sT_ready{d}") for d in range(2)]
        st_copied = [sem(f"st_copied{d}") for d in range(2)]
        agg_ready = sem("agg_ready")
        hx_in = sem("hx_in")
        rwT_ready = sem("rwT_ready")
        rwT_copied = sem("rwT_copied")
        a_step = sem("a_step")
        staged = sem("staged")
        xn_staged = sem("xn_staged")
        block_done = sem("block_done")
        ffw_in = sem("ffw_in")
        b1_in = sem("b1_in")
        mask_ready = sem("mask_ready")
        xT_ready = sem("xT_ready")
        xT_copied = sem("xT_copied")
        logits_ready = sem("logits_ready")
        pick_ready = sem("pick_ready")
        ohT_ready = sem("ohT_ready")
        ohT_copied = sem("ohT_copied")
        hid_ready = sem("hid_ready")
        hid_copied = sem("hid_copied")
        ff_ready = sem("ff_ready")
        f_step = sem("f_step")
        out_ready = sem("out_ready")
        out_done = sem("out_done")

        tot_ps = ps[0][:, 0:2 * NBLK]
        base_ps = ps[0][:, 512:512 + 2 * NBLK]

        block = ctx.enter_context(nc.Block())

        @block.sync
        def _(sp):
            for i, k in ((TO, dst), (FROM, src)):
                sp.dma_start(keys[0:RP, i * RC:(i + 1) * RC],
                             k.rearrange("(p c) -> p c", c=RC)).then_inc(keys_in, 16)
            xs = x_sb.rearrange("p (b d) -> p b d", b=NBLK)
            sp.wait_ge(const_ready, 1)
            sp.dma_start(xs[:, 0:NBLK - 1, :],
                         x[0:(NBLK - 1) * P, :].rearrange("(b p) d -> p b d", p=P)).then_inc(x_in, 16)
            sp.dma_start(xs[0:TAIL, NBLK - 1, :], x[(NBLK - 1) * P:N, :]).then_inc(x_in, 16)
            wr = w_raw.rearrange("p (d o i) -> p d o i", d=2, o=2)
            for i, w in ((TO, w_fwd), (FROM, w_back)):
                sp.dma_start(wr[:, i], w.rearrange("(o p) i -> p o i", p=P)).then_inc(w_in, 16)
            sp.wait_ge(tinit_ready, 1)
            sp.dma_start(t_dram.rearrange("(p t) f -> p (t f)", p=P), t_init).then_inc(tinit_out, 16)
            sp.wait_ge(h_ready, 1)
            sp.dma_start(h_dram.rearrange("(b p) d -> p b d", p=P),
                         h_sb.rearrange("p (b d) -> p b d", b=NBLK)).then_inc(h_out, 16)
            sp.wait_ge(meta_out, 16 * 2 * RC)
            sp.dma_start(table[:, :], t_dram.rearrange("(p t) f -> p (t f)", p=P)).then_inc(table_in, 16)
            sp.wait_ge(loop_done, 1)
            for r, v in ((bf_r, b_fwd), (bb_r, b_back), (ga_r, gamma), (be_r, beta), (rb_r, router_b)):
                sp.dma_start(r, v.rearrange("(a n) -> a n", a=1).broadcast_to([P, v.shape[0]])).then_inc(rows_in, 16)
            sp.dma_start(rw_raw, router_w[:, :]).then_inc(rows_in, 16)
            sp.dma_start(b2_s, b2[:, :]).then_inc(rows_in, 16)
            sp.wait_ge(h_out, 16)
            with sp.Fori(0, NBLK - 1) as b:
                sp.wait_ge(block_done, b)
                sp.dma_start(v_h, h_dram[bass.ds(b * P, P), :]).then_inc(hx_in, 16)
                sp.dma_start(xin, x[bass.ds(b * P, P), :]).then_inc(hx_in, 16)
            sp.wait_ge(block_done, NBLK - 1)
            sp.dma_start(v_h, h_dram[(NBLK - 1) * P:NBLK * P, :]).then_inc(hx_in, 16)
            sp.dma_start(xin[0:TAIL, :], x[(NBLK - 1) * P:N, :]).then_inc(hx_in, 16)
            sp.wait_ge(block_done, NBLK)
            w1_v = w1.rearrange("(c e) (k p) h -> p c e k h", e=2, p=P)
            for c in range(UC):
                for k in range(2):
                    sp.dma_start(S[:, c, 2 * D + k * P:2 * D + (k + 1) * P].rearrange("p (e h) -> p e h", e=2),
                                 w1_v[:, c, :, k, :]).then_inc(ffw_in, 16)
            sp.dma_start(S[:, 0:UC, 3 * D:4 * D],
                         w2.rearrange("(c e) h n -> (e h) c n", e=2)).then_inc(ffw_in, 16)
            sp.dma_start(b1_b, b1.rearrange("(a e) h -> a (e h)", a=1).broadcast_to([NX, NX * NH])).then_inc(b1_in, 16)
            with sp.Fori(0, NBLK - 1) as b:
                sp.wait_ge(out_ready, b + 1)
                sp.dma_start(out[bass.ds(b * P, P), :], ff_o).then_inc(out_done, 16)
            sp.wait_ge(out_ready, NBLK)
            sp.dma_start(out[(NBLK - 1) * P:N, :], ff_o[0:TAIL, :]).then_inc(out_done, 16)
            sp.wait_ge(out_done, 16 * NBLK)

        @block.gpsimd
        def _(g):
            g.memset(x_sb.rearrange("p (b d) -> p b d", b=NBLK)[:, NBLK - 1, :], 0.0).then_inc(const_ready, 1)
            g.iota(iota_f[:, :], pattern=[[1, P]], base=0, channel_multiplier=0,
                   allow_small_or_imprecise_dtypes=True).then_inc(const_ready, 1)
            g.iota(tile_n, pattern=[[1, TILES]], base=0, channel_multiplier=0,
                   allow_small_or_imprecise_dtypes=True).then_inc(const_ready, 1)
            g.memset(ident[:, :], 0.0).then_inc(const_ready, 1)
            g.memset(before[:, :], 1.0).then_inc(const_ready, 1)
            g.memset(ones_m[:, :], 1.0).then_inc(const_ready, 1)
            g.memset(ones_r, 1.0).then_inc(const_ready, 1)
            g.memset(PRv[:, :, :, D:D + 1], 1.0).then_inc(const_ready, 1)
            g.wait_ge(const_ready, 8)
            g.affine_select(out=ident[:, :], in_=ident[:, :], compare_op=ALU.not_equal, fill=1.0, base=0,
                            pattern=[[-1, P]], channel_multiplier=1).then_inc(const_ready, 1)
            g.affine_select(out=before[:, :], in_=before[:, :], compare_op=ALU.is_gt, fill=0.0, base=0,
                            pattern=[[1, P]], channel_multiplier=-1).then_inc(const_ready, 1)
            ti = t_init.rearrange("p (t f) -> p t f", f=3)
            g.memset(ti[:, :, 0:2], 0).then_inc(const_ready, 1)
            g.memset(ti[:, :, 2:3], -1).then_inc(const_ready, 1)
            g.wait_ge(const_ready, 12)
            g.nop().then_inc(tinit_ready, 1)
            mt = meta.rearrange("p (d c f) -> p d c f", d=2, f=3)
            for d in range(2):
                g.iota(mt[0:RP, d, :, 0], pattern=[[1, RC]], base=0, channel_multiplier=RC).then_inc(meta_id, 1)
            g.wait_ge(tinit_out, 16)
            g.wait_ge(meta_id, 2)
            g.wait_ge(pos_ready, 1)
            for d in range(2):
                for c in range(RC):
                    g.indirect_dma_start(
                        out=t_dram[:, :], out_offset=bass.IndirectOffsetOnAxis(
                            ap=row_id[0:RP, d * RC + c:d * RC + c + 1], axis=0),
                        in_=mt[0:RP, d, c, :], in_offset=None).then_inc(meta_out, 16)
            g.wait_ge(h_out, 16)
            g.wait_ge(wt_read, 6)
            g.wait_ge(idx_first, 2)
            with g.Fori(0, GROUPS) as k:
                for u in range(UNROLL):
                    for d in range(2):
                        g.wait_ge(const_ready, 12)
                        if u % 2 == 0 and d == 0:
                            g.wait_ge(idx_ready[u // 2], k)
                        g.wait_ge(mm_done[d][u], k)
                        for f, table_rows in ((0, edge), (1, h_dram)):
                            g.indirect_dma_start(
                                out=Xv[:, d, u, (1 - f) * D:(2 - f) * D], out_offset=None,
                                in_=table_rows[:, :], in_offset=bass.IndirectOffsetOnAxis(
                                    ap=IDv[:, u // 2, u % 2, d, f:f + 1], axis=0)).then_inc(got[d][u], 16)
            g.wait_ge(b1_in, 16)
            bb = b1_b.rearrange("p (e h) -> p e h", e=NX)
            g.affine_select(out=bb, in_=bb, compare_op=ALU.is_equal, fill=NEVER, base=0,
                            pattern=[[1, NX], [0, NH]], channel_multiplier=-1).then_inc(mask_ready, 1)

        @block.scalar
        def _(a):
            a.wait_ge(var_ready, 1)
            a.activation(sm(1, NBLK), sm(0, NBLK), ACT.Sqrt).then_inc(std_ready, 1)
            for i in range(6):
                a.wait_ge(wt_ready, i + 1)
                a.activation(w_gnn[:, i * 2 * D:(i + 1) * 2 * D], ps[1 + i % 3][:, 0:2 * D], ACT.Copy).then_inc(wt_read, 1)
            tb = table[:, :].rearrange("p (t d f) -> p t d f", d=2, f=3)
            a.wait_ge(table_in, 16)
            for h in range(2):
                a.activation(IDv[:, h], tb[:, 2 * h:2 * h + 2, :, 0:2], ACT.Copy).then_inc(idx_first, 1)
            with a.Fori(1, GROUPS) as k:
                for h in range(2):
                    for u in (2 * h, 2 * h + 1):
                        for d in range(2):
                            a.wait_ge(got[d][u], k * 32)
                    a.activation(IDv[:, h], tb[:, bass.ds(k * UNROLL + 2 * h, 2), :, 0:2],
                                 ACT.Copy).then_inc(idx_ready[h], 1)
            a.wait_ge(loop_done, 1)
            with a.Fori(0, NBLK) as b:
                a.wait_ge(sT_ready[1], b)
                a.activation(stage, arena[:, bass.ds(b * SB, SB)], ACT.Copy).then_inc(staged, 1)
                a.wait_ge(sT_ready[0], b + 1)
                a.wait_ge(agg_ready, b)
                a.activation(ST[:, 0], ps[0][:, 0:6 * P].rearrange("p (k n) -> p k n", k=6),
                             ACT.Copy).then_inc(st_copied[0], 1)
                for i in range(2):
                    a.wait_ge(var_ready, 2 * b + i + 2)
                    a.activation(sm(3, 1), sm(2, 1), ACT.Sqrt).then_inc(std_ready, 1)
            a.wait_ge(block_done, NBLK)
            with a.Fori(0, NBLK) as b:
                a.wait_ge(xT_ready, b)
                a.activation(xn_c, arena[:, bass.ds(b * SB + D, D)], ACT.Copy).then_inc(xn_staged, 1)
                for q in range(UC // 4):
                    a.wait_ge(hid_ready, b * (UC // 4) + q + 1)
                    if q == 0:
                        a.wait_ge(ff_ready, b)
                    a.activation(hid[:, q * 4 * P:(q + 1) * 4 * P], ps[1 + q % 2][:, 0:512],
                                 ACT.Relu).then_inc(hid_copied, 1)

        @block.vector
        def _(v):
            steps = [0]

            def done(ins):
                steps[0] += 1
                ins.then_inc(v_step, 1)
                v.wait_ge(v_step, steps[0])

            kd = keys[0:RP, :]
            v.wait_ge(keys_in, 32)
            done(v.tensor_scalar(blk_i[0:RP, :], kd, 7, None, ALU.logical_shift_right))
            done(v.tensor_scalar(low_i[0:RP, :], kd, P - 1, None, ALU.bitwise_and))
            done(v.tensor_copy(blk_h[0:RP, :], blk_i[0:RP, :]))
            mt = meta.rearrange("p (d c f) -> p d c f", d=2, f=3)
            for d in range(2):
                done(v.tensor_copy(mt[0:RP, d, :, 1], keys[0:RP, (1 - d) * RC:(2 - d) * RC]))
                done(v.tensor_copy(mt[0:RP, d, :, 2], low_i[0:RP, d * RC:(d + 1) * RC]))
            v.wait_ge(const_ready, 12)
            cnt = sm(4)
            with v.Fori(0, NBLK) as b:
                for d in range(2):
                    ins = v.tensor_scalar(member[0:RP, bass.ds((b * 2 + d) * RC, RC)], blk_h[0:RP, d * RC:(d + 1) * RC],
                                          iota_f[0:RP, bass.ds(b, 1)], 0.0, ALU.is_equal, ALU.add,
                                          accum_out=cnt[0:RP, bass.ds(b * 2 + d, 1)])
                    ins.then_inc(cmp_done, 1)
            v.wait_ge(cmp_done, 2 * NBLK)
            v.nop().then_inc(counts_ready, 1)
            v.wait_ge(x_in, 32)
            xs = x_sb.rearrange("p (b d) -> p b d", b=NBLK)
            hs = h_sb.rearrange("p (b d) -> p b d", b=NBLK)
            st6 = sm(8, 6 * NBLK)
            mv = sm(12, 2 * NBLK)
            for b in range(NBLK):
                v.bn_stats(st6[:, 6 * b:6 * b + 6], xs[:, b, :]).then_inc(tb_done, 1)
            v.wait_ge(tb_done, NBLK)
            for b in range(NBLK):
                v.bn_aggr(mv[:, 2 * b:2 * b + 2], st6[:, 6 * b:6 * b + 6]).then_inc(tb_done, 1)
            v.wait_ge(tb_done, 2 * NBLK)
            mv2 = mv.rearrange("p (b t) -> p b t", t=2)
            v.tensor_scalar(sm(0, NBLK), mv2[:, :, 1], EPS, None, ALU.add).then_inc(var_ready, 1)
            v.wait_ge(std_ready, 1)
            done(v.reciprocal(sm(0, NBLK), sm(1, NBLK)))
            for b in range(NBLK):
                v.tensor_scalar(hs[:, b, :], xs[:, b, :], mv2[:, b, 0:1], sm(0, NBLK)[:, b:b + 1],
                                ALU.subtract, ALU.mult).then_inc(tb_done, 1)
            v.wait_ge(tb_done, 3 * NBLK)
            v.nop().then_inc(h_ready, 1)
            v.wait_ge(base_ready, 1)
            done(v.tensor_scalar(sm(5, dt=I32), tot_ps, float(P - 1), None, ALU.add))
            done(v.tensor_scalar(sm(6, dt=I32), sm(5, dt=I32), 7, None, ALU.logical_shift_right))
            tiles_f, tend, off = sm(7), sm(14), sm(15)
            tl = tiles_f.rearrange("p (d b) -> p d b", d=2)
            te = tend.rearrange("p (d b) -> p d b", d=2)
            done(v.tensor_copy(tl, sm(6, dt=I32).rearrange("p (b d) -> p d b", d=2)))
            for d in range(2):
                done(v.tensor_tensor_scan(te[:, d, :], ones_m[:, 0:NBLK], tl[:, d, :], 0.0, ALU.mult, ALU.add))
            done(v.tensor_tensor(tiles_f, tend, tiles_f, ALU.subtract))
            done(v.tensor_scalar(tiles_f, tiles_f, float(P), -1.0, ALU.mult, ALU.add))
            done(v.tensor_tensor(off.rearrange("p (d b) -> p d b", d=2)[0:RP],
                                 base_ps.rearrange("p (b d) -> p d b", d=2)[0:RP],
                                 tl[0:RP], ALU.add))
            done(v.memset(pos[0:RP, :], 0.0))
            with v.Fori(0, NBLK) as b:
                b1 = v.snap(b + 1)
                for d in range(2):
                    mem = member[0:RP, bass.ds((b * 2 + d) * RC, RC)]
                    rk = rank[0:RP, d * RC:(d + 1) * RC]
                    v.wait_ge(pick_done[d], b)
                    v.tensor_tensor_scan(rk, ones_r[0:RP, :], mem, off[0:RP, bass.ds(b + d * NBLK, 1)],
                                         ALU.mult, ALU.add).then_inc(scan_done[d], 1)
                for d in range(2):
                    mem = member[0:RP, bass.ds((b * 2 + d) * RC, RC)]
                    rk = rank[0:RP, d * RC:(d + 1) * RC]
                    v.wait_ge(scan_done[d], b1)
                    v.tensor_tensor(rk, rk, mem, ALU.mult).then_inc(rank_masked[d], 1)
                for d in range(2):
                    rk, ps_ = rank[0:RP, d * RC:(d + 1) * RC], pos[0:RP, d * RC:(d + 1) * RC]
                    v.wait_ge(rank_masked[d], b1)
                    v.tensor_tensor(ps_, ps_, rk, ALU.add).then_inc(pick_done[d], 1)
            for d in range(2):
                v.wait_ge(pick_done[d], NBLK)
            done(v.tensor_copy(pos_i[0:RP, :], pos[0:RP, :]))
            done(v.tensor_scalar(row_i[0:RP, :], pos_i[0:RP, :], P - 1, None, ALU.bitwise_and))
            done(v.tensor_scalar(col_i[0:RP, :], pos_i[0:RP, :], 7, None, ALU.logical_shift_right))
            done(v.scalar_tensor_tensor(pos[0:RP, :], row_i[0:RP, :], float(TILES), col_i[0:RP, :], ALU.mult, ALU.add))
            for d in range(2):
                done(v.tensor_scalar(row_id[0:RP, d * RC:(d + 1) * RC], pos[0:RP, d * RC:(d + 1) * RC],
                                     2.0, float(d), ALU.mult, ALU.add))
            v.nop().then_inc(pos_ready, 1)
            done(v.memset(tile_blk[:, :], 0.0))
            tbv = tile_blk[:, :].rearrange("p (t d) -> p t d", d=2)
            with v.Fori(0, NBLK - 1) as b:
                for d in range(2):
                    v.wait_ge(tb_done, 3 * NBLK + 2 * b + d)
                    v.scalar_tensor_tensor(tbv[:, :, d], tile_n[0:1, :], tend[0:1, bass.ds(b + d * NBLK, 1)],
                                           tbv[:, :, d], ALU.is_ge, ALU.add).then_inc(tb_done, 1)
            v.wait_ge(tb_done, 3 * NBLK + 2 * (NBLK - 1))
            done(v.tensor_copy(tile_blk_i[:, :], tile_blk[:, :]))
            v.nop().then_inc(blk_ready, 1)
            v.wait_ge(w_in, 32)
            wr = w_raw.rearrange("p (d o i) -> p (d o) i", d=2, o=2)
            for part in range(2):
                w = wr[:, :, part * D:(part + 1) * D]
                v.tensor_tensor(w, w, wr[:, :, 2 * D:3 * D], ALU.add).then_inc(wsum_ready, 1)
            v.wait_ge(meta_out, 16 * 2 * RC)
            v.wait_ge(h_out, 16)
            v.wait_ge(tinit_out, 16)
            v.wait_ge(wt_read, 6)
            done(v.memset(arena[:, :], 0.0))

            v.wait_ge(table_in, 16)
            with v.Fori(0, GROUPS) as k:
                _, blocks = nc.values_load_multi_w_load_instructions(
                    tile_blk_i[0:1, bass.ds(k * 2 * UNROLL, 2 * UNROLL)], engines=[mybir.EngineType.DVE],
                    min_val=0, max_val=NBLK - 1,
                    skip_runtime_bounds_check_because="a count of at most NBLK - 1 comparisons that hold")

                def operands(u):
                    for d in range(2):
                        if u >= 2:
                            v.wait_ge(mm_done[d][u - 2], k + 1)
                        else:
                            v.wait_ge(mm_done[d][u + 2], k)
                        key = table[:, bass.ds((k * UNROLL + u) * 6 + d * 3 + 2, 1)]
                        v.tensor_scalar(OHv[:, d, u % 2, :], iota_f[:, :], key, None,
                                        ALU.is_equal).then_inc(rhs_ready[d][u], 1)
                        v.wait_ge(got[d][u], 32 * (k + 1))
                        v.tensor_tensor(PRv[:, d, u % 2, 0:D], Xv[:, d, u, 0:D], Xv[:, d, u, D:2 * D],
                                        ALU.mult).then_inc(rhs_ready[d][u], 1)

                def add(u):
                    for d in range(2):
                        sums = arena[:, bass.ds(blocks[2 * u + d] * SB + d * SW, SW)]
                        v.wait_ge(mm_done[d][u], k + 1)
                        v.wait_ge(summed[d], k * UNROLL + u)
                        v.tensor_tensor(sums, sums, ps[2 * d + u % 2][:, 0:SW], ALU.add).then_inc(summed[d], 1)

                operands(0)
                for u in range(1, UNROLL):
                    operands(u)
                    add(u - 1)
                add(UNROLL - 1)
            for d in range(2):
                v.wait_ge(summed[d], TILES)
            v.nop().then_inc(loop_done, 1)

            v.wait_ge(rows_in, 16 * 7)
            v.wait_ge(rwT_ready, 1)
            done(v.tensor_copy(rwT, ps[3][:, 512:512 + 2 * NX]))
            v.nop().then_inc(rwT_copied, 1)
            PER = 16
            with v.Fori(0, NBLK) as b:
                n = [0]

                def then(ins, own=None):
                    if own is None:
                        n[0] += 1
                        ins.then_inc(a_step, 1)
                        v.wait_ge(a_step, b * PER + n[0])
                    else:
                        ins.then_inc(own, 1)
                        v.wait_ge(const_ready, 12)
                        v.wait_ge(own, b1)

                b1 = v.snap(b + 1)
                v.wait_ge(sT_ready[1], b1)
                v.wait_ge(agg_ready, b)
                v.tensor_copy(ST[:, 1], ps[1][:, 0:6 * P].rearrange("p (k n) -> p k n", k=6)).then_inc(st_copied[1], 1)
                cf = arena[:, bass.ds(b * SB + SW - 1, 1)]
                cb = arena[:, bass.ds(b * SB + 2 * SW - 1, 1)]
                x1 = arena[:, bass.ds(b * SB, D)]
                xn = arena[:, bass.ds(b * SB + D, D)]
                then(v.tensor_tensor(sm(16, 1), cf, cb, ALU.add))
                then(v.tensor_scalar(sm(16, 1), sm(16, 1), 1.0, None, ALU.max))
                then(v.reciprocal(sm(16, 1), sm(16, 1)))
                v.wait_ge(agg_ready, b + 1)
                then(v.scalar_tensor_tensor(v_a, bf_r, cf, ps[2][:, 0:D], ALU.mult, ALU.add))
                then(v.scalar_tensor_tensor(v_a, bb_r, cb, v_a, ALU.mult, ALU.add))
                then(v.tensor_scalar(v_a, v_a, sm(16, 1), None, ALU.mult))
                then(v.scalar_tensor_tensor(v_a, v_a, SLOPE, v_a, ALU.mult, ALU.max))
                v.wait_ge(hx_in, 32 * (b + 1))
                then(v.tensor_tensor(v_a, v_a, v_h, ALU.add))
                then(v.bn_stats(sm(17, 6), v_a), own[0])
                then(v.bn_aggr(sm(18, 2), sm(17, 6)))
                v.tensor_scalar(sm(2, 1), sm(18, 2)[:, 1:2], EPS, None, ALU.add).then_inc(var_ready, 1)
                v.wait_ge(std_ready, 2 * b + 2)
                then(v.reciprocal(sm(19, 1), sm(3, 1)))
                then(v.tensor_scalar(v_a, v_a, sm(18, 2)[:, 0:1], sm(19, 1), ALU.subtract, ALU.mult))
                then(v.tensor_tensor(v_a, v_a, ga_r, ALU.mult))
                then(v.tensor_tensor(v_a, v_a, be_r, ALU.add))
                then(v.tensor_tensor(x1, v_a, xin, ALU.add), own[1])
                then(v.bn_stats(sm(17, 6), x1), own[2])
                then(v.bn_aggr(sm(18, 2), sm(17, 6)))
                v.tensor_scalar(sm(2, 1), sm(18, 2)[:, 1:2], EPS, None, ALU.add).then_inc(var_ready, 1)
                v.wait_ge(std_ready, 2 * b + 3)
                then(v.reciprocal(sm(19, 1), sm(3, 1)))
                then(v.tensor_scalar(xn, x1, sm(18, 2)[:, 0:1], sm(19, 1), ALU.subtract, ALU.mult))
                v.nop().then_inc(block_done, 1)
                assert n[0] == PER

            PER_F = 4
            with v.Fori(0, NBLK) as b:
                x1 = arena[:, bass.ds(b * SB, D)]
                n2 = [0]

                def thenf(ins, own=None):
                    if own is None:
                        n2[0] += 1
                        ins.then_inc(f_step, 1)
                        v.wait_ge(f_step, b * PER_F + n2[0])
                    else:
                        ins.then_inc(own, 1)
                        v.wait_ge(const_ready, 12)
                        v.wait_ge(own, b1)

                b1 = v.snap(b + 1)
                v.wait_ge(xT_ready, b1)
                v.wait_ge(ff_ready, b)
                v.tensor_copy(xT, ps[0][:, 0:2 * P]).then_inc(xT_copied, 1)
                v.wait_ge(logits_ready, b + 1)
                thenf(v.tensor_tensor(lg, ps[0][:, 512:512 + NX], rb_r, ALU.add), own[3])
                thenf(v.max(mx8, lg), own[4])
                thenf(v.max_index(mi8, mx8, lg))
                thenf(v.tensor_copy(mif, mi8[:, 0:1]))
                thenf(v.tensor_scalar(oh, iota_f[:, 0:NX], mif, None, ALU.is_equal))
                v.nop().then_inc(pick_ready, 1)
                v.wait_ge(ohT_ready, b + 1)
                v.tensor_copy(ohT, ps[0][0:NX, 640:640 + P]).then_inc(ohT_copied, 1)
                v.wait_ge(ff_ready, b + 1)
                v.wait_ge(out_done, 16 * b)
                thenf(v.scalar_tensor_tensor(ff_o, ps[3][:, 0:D], 0.0, x1, ALU.max, ALU.add))
                v.nop().then_inc(out_ready, 1)
                assert n2[0] == PER_F

        @block.tensor
        def _(pe):
            pe.wait_ge(const_ready, 12)
            pe.wait_ge(counts_ready, 1)
            cnt = sm(4)
            nc.tensor.matmul(tot_ps, ones_m[0:RP, :], cnt[0:RP, :], start=True, stop=True)
            nc.tensor.matmul(base_ps, before[0:RP, :], cnt[0:RP, :], start=True, stop=True).then_inc(base_ready, 1)
            pe.wait_ge(wsum_ready, 2)
            ws = w_raw.rearrange("p (d o i) -> p d o i", d=2, o=2)
            for i in range(6):
                if i >= 3:
                    pe.wait_ge(wt_read, i - 2)
                for j in range(2):
                    d, kk = (2 * i + j) // 6, (2 * i + j) % 6
                    col = kk * P if kk < 4 else (kk + 2) * P
                    for o in range(2):
                        last = nc.tensor.transpose(ps[1 + i % 3][:, (2 * j + o) * P:(2 * j + o + 1) * P],
                                                   ws[:, d, o, col:col + P], ident[:, :])
                last.then_inc(wt_ready, 1)
            pe.wait_ge(wt_read, 6)
            with pe.Fori(0, GROUPS) as k:
                for u in range(UNROLL):
                    for d in range(2):
                        pe.wait_ge(rhs_ready[d][u], 2 * (k + 1))
                        if u >= 2:
                            pe.wait_ge(summed[d], k * UNROLL + u - 1)
                        else:
                            pe.wait_ge(summed[d], k * (UNROLL) - (1 - u) * 1 if False else k * UNROLL)
                        a = ps[2 * d + u % 2]
                        nc.tensor.matmul(a[:, 0:512], OHv[:, d, u % 2, :], Xv[:, d, u, :], start=True, stop=True)
                        nc.tensor.matmul(a[:, 512:SW], OHv[:, d, u % 2, :], PRv[:, d, u % 2, :], start=True,
                                         stop=True).then_inc(mm_done[d][u], 1)
            pe.wait_ge(loop_done, 1)
            pe.wait_ge(rows_in, 16 * 7)
            for kk in range(2):
                last = nc.tensor.transpose(ps[3][:, 512 + kk * NX:512 + (kk + 1) * NX],
                                           rw_raw[:, kk * P:(kk + 1) * P], ident[0:NX, 0:NX])
            last.then_inc(rwT_ready, 1)
            with pe.Fori(0, NBLK) as b:
                pe.wait_ge(staged, b + 1)
                for d in range(2):
                    pe.wait_ge(st_copied[d], b)
                    for kk in range(6):
                        last = nc.tensor.transpose(ps[d][:, kk * P:(kk + 1) * P],
                                                   stage[:, d * SW + kk * P:d * SW + (kk + 1) * P], ident[:, :])
                    last.then_inc(sT_ready[d], 1)
                pe.wait_ge(block_done, b)
                for d in range(2):
                    pe.wait_ge(st_copied[d], b + 1)
                    for kk in range(6):
                        last = nc.tensor.matmul(ps[2][:, 0:D], ST[:, d, kk, :],
                                                w_gnn[:, (d * 6 + kk) * D:(d * 6 + kk + 1) * D],
                                                start=(d == 0 and kk == 0), stop=(d == 1 and kk == 5))
                last.then_inc(agg_ready, 1)
            pe.wait_ge(rwT_copied, 1)
            pe.wait_ge(block_done, NBLK)
            pe.wait_ge(ffw_in, 16 * (2 * UC + 1))
            pe.wait_ge(mask_ready, 1)
            with pe.Fori(0, NBLK) as b:
                pe.wait_ge(xn_staged, b + 1)
                for kk in range(2):
                    last = nc.tensor.transpose(ps[0][:, kk * P:(kk + 1) * P],
                                               xn_c[:, kk * P:(kk + 1) * P], ident[:, :])
                last.then_inc(xT_ready, 1)
                pe.wait_ge(xT_copied, b + 1)
                for kk in range(2):
                    last = nc.tensor.matmul(ps[0][:, 512:512 + NX], xT[:, kk * P:(kk + 1) * P],
                                            rwT[:, kk * NX:(kk + 1) * NX], start=(kk == 0), stop=(kk == 1))
                last.then_inc(logits_ready, 1)
                pe.wait_ge(pick_ready, b + 1)
                nc.tensor.transpose(ps[0][0:NX, 640:640 + P], oh, ident[:, :]).then_inc(ohT_ready, 1)
                pe.wait_ge(ohT_copied, b + 1)
                for q in range(UC // 4):
                    pe.wait_ge(hid_copied, b * (UC // 4) + max(q - 1, 0))
                    for c in range(4 * q, 4 * q + 4):
                        o = ps[1 + q % 2][:, (c % 4) * P:(c % 4 + 1) * P]
                        nc.tensor.matmul(o, b1_b[:, c * P:(c + 1) * P], ohT, start=True, stop=False)
                        for kk in range(2):
                            last = nc.tensor.matmul(o, S[:, c, 2 * D + kk * P:2 * D + (kk + 1) * P],
                                                    xT[:, kk * P:(kk + 1) * P], start=False, stop=(kk == 1))
                    last.then_inc(hid_ready, 1)
                pe.wait_ge(out_ready, b)
                nc.tensor.matmul(ps[3][:, 0:D], ohT, b2_s, start=True, stop=False)
                for q in range(UC // 4):
                    pe.wait_ge(hid_copied, b * (UC // 4) + q + 1)
                    for c in range(4 * q, 4 * q + 4):
                        last = nc.tensor.matmul(ps[3][:, 0:D], hid[:, c * P:(c + 1) * P], S[:, c, 3 * D:4 * D],
                                                start=False, stop=(c == UC - 1))
                last.then_inc(ff_ready, 1)


_INS = ['x', 'src', 'dst', 'edge_attr_256', 'L0_gnn_W_fwd', 'L0_gnn_b_fwd', 'L0_gnn_W_back', 'L0_gnn_b_back',
        'L0_gnn_gamma', 'L0_gnn_beta', 'L0_ffn_router_w', 'L0_ffn_router_b', 'L0_ffn_W1', 'L0_ffn_b1',
        'L0_ffn_W2', 'L0_ffn_b2']


def kernel(**inputs):
    import numpy as _np
    import concourse.bacc as _bacc
    from concourse import mybir as _mybir
    from concourse.bass_utils import run_bass_kernel_spmd as _run

    nc = _bacc.Bacc("TRN2", target_bir_lowering=False, num_devices=1)
    arrays, args = {}, []
    for name in _INS:
        a = _np.ascontiguousarray(inputs[name])
        arrays[f"in_{name}_dram"] = a
        args.append(nc.dram_tensor(f"in_{name}_dram", a.shape, _mybir.dt.from_np(a.dtype), kind="ExternalInput").ap())
    out = nc.dram_tensor("out_0_dram", (N, D), _mybir.dt.float32, kind="ExternalOutput").ap()
    gnn_ffn(nc, *args, out)
    r = _run(nc, [arrays], core_ids=[0])
    return r.results[0]["out_0_dram"]
```

```python
import concourse.bass as bass
from concourse import mybir
from contextlib import ExitStack

F32, I32, U16, BF16 = mybir.dt.float32, mybir.dt.int32, mybir.dt.uint16, mybir.dt.bfloat16
ALU = mybir.AluOpType
ACT = mybir.ActivationFunctionType
AX = mybir.AxisListType

P = 128
N, D = 3125, 256
E = 53125
RP, RC = 125, 425
NBLK = (N + P - 1) // P
TAIL = N - (NBLK - 1) * P
UNROLL = 4
TILES = -(-((E + NBLK * (P - 1)) // P) // UNROLL) * UNROLL
GROUPS = TILES // UNROLL
SLOTS = P * TILES
SW = 3 * D + 1
SB = 2 * SW
NX, NH, SLOPE, EPS = 32, 64, 0.01, 1e-5
FT = (N + NX * (P - 1)) // P
W_AT = 2 * D
W_LEN = 2 * NH + D
B1_AT = W_AT + 2 * W_LEN
NONE = -1048576.0
TO, FROM = 0, 1


def gnn_ffn(nc, x, src, dst, edge, w_fwd, b_fwd, w_back, b_back, gamma, beta,
            router_w, router_b, w1, b1, w2, b2, out):
    assert RP * RC == E and FT % 2 == 0 and B1_AT + 2 * NH <= SB and NX // 2 <= NBLK
    ctx = ExitStack()
    with ctx:
        def sb(name, cols, dt=F32, rows=P):
            return ctx.enter_context(nc.sbuf_tensor(name, [rows, cols], dt))

        def sem(name):
            return ctx.enter_context(nc.semaphore(name))

        def dram(name, shape, dt=F32):
            return nc.dram_tensor(name, shape, dt, kind="Internal").ap()

        h_dram = dram("h_rows", (NBLK * P, D))
        to_dram = dram("to_table", (SLOTS + E, 3), I32)
        from_dram = dram("from_table", (SLOTS, 3), I32)
        xs_dram = dram("rows_by_expert", (FT * P, D))
        ys_dram = dram("outputs_by_expert", (FT * P, D))

        arena = sb("arena", NBLK * SB)
        at = [0]

        def carve(cols, dt=F32):
            words = cols if dt in (F32, I32) else (cols + 1) // 2
            a = at[0]
            at[0] = a + words
            assert at[0] <= NBLK * SB
            v = arena[:, a:a + words]
            return v if dt == F32 else v.bitcast(dt)

        x_sb = carve(NBLK * D)
        h_sb = carve(NBLK * D)
        keys = carve(2 * RC, I32)
        next_i = carve(RC, I32)
        blk_i = carve(2 * RC, I32)
        low_i = carve(2 * RC, I32)
        blk_h = carve(2 * (RC + 1), BF16)
        ones_r = carve(RC)
        rank = carve(2 * RC)
        pos = carve(RC)
        pos_i = carve(RC, I32)
        row_i = carve(RC, I32)
        col_i = carve(RC, I32)
        slot_id = carve(2 * RC, I32)
        member = carve(NBLK * RC, U16)
        meta = carve(2 * RC * 3, I32)
        to_init = carve(TILES * 3, I32)
        tile_n = carve(TILES)
        tile_b = carve(2 * TILES)
        step_t = carve(TILES)
        delta_t = carve(TILES)
        rows_f = carve(2 * TILES)
        sorted_f = carve(4)
        S = arena[:, :].rearrange("p (b w) -> p b w", b=NBLK)

        w_gnn = sb("w_gnn", 2 * 6 * D)
        table = sb("table", TILES * 3, I32)
        X = sb("X", 2 * UNROLL * 2 * D)
        PROH = sb("PROH", 2 * 2 * (D + 1) + 2 * 2 * P)
        PR = PROH[:, 0:2 * 2 * (D + 1)]
        OH = PROH[:, 2 * 2 * (D + 1):]
        stage = PROH[:, 0:SB]
        idx = sb("idx", 2 * 2 * 2, I32)
        ring = sb("ring", UNROLL * 3, I32)
        late = sb("late", UNROLL)
        key_to = sb("key_to", UNROLL)
        first_e = sb("first_e", TILES)
        neg_blk = sb("neg_blk", TILES)
        iota_f = sb("iota_f", P)
        ident = sb("ident", P)
        before = sb("before", P)
        ones_m = sb("ones_m", P)
        small = sb("small", 18 * 2 * NBLK)
        tile_blk_i = sb("tile_blk_i", 2 * TILES, I32, 1)
        tile_rows_i = sb("tile_rows_i", 2 * TILES, I32, 1)
        flag_i = sb("flag_i", 1, I32, 1)
        t_init = table[:, :]
        w_raw = X[:, 0:2 * 2 * 4 * D]
        Xv = X[:, :].rearrange("p (d u w) -> p d u w", d=2, u=UNROLL)
        PRv = PR.rearrange("p (d u w) -> p d u w", d=2, u=2)
        OHv = OH.rearrange("p (d u w) -> p d u w", d=2, u=2)
        IDv = idx[:, :].rearrange("p (h u f) -> p h u f", h=2, u=2)
        RG = ring[:, :].rearrange("p (u f) -> p u f", u=UNROLL)

        def sm(i, cols=2 * NBLK, dt=F32):
            v = small[:, i * 2 * NBLK:i * 2 * NBLK + cols]
            return v if dt == F32 else v.bitcast(dt)

        ST = X[:, 0:2 * 6 * P].rearrange("p (d k n) -> p d k n", d=2, k=6)
        free = X[:, 2 * 6 * P:]
        v_a, v_h, xin, xn_c, xT = (free[:, i * D:(i + 1) * D] for i in range(5))
        bf_r, bb_r, ga_r, be_r = (free[:, (5 + i) * D:(6 + i) * D] for i in range(4))
        rows = table[:, :].bitcast(F32)
        rb_r = rows[:, 0:NX]
        rwT = rows[:, NX:3 * NX]
        rw_raw = rows[0:NX, 3 * NX:3 * NX + D]
        lg = rows[:, 400:400 + NX]
        mx8 = rows[:, 440:448]
        mi8 = rows[:, 448:456].bitcast(mybir.dt.uint32)
        eid = rows[:, 460:460 + NBLK]
        valid = rows[:, 490:491]
        slot_x = rows[:, 500:500 + NBLK]
        slot_xi = rows[:, 530:530 + NBLK].bitcast(I32)
        ex = [rows[:, 560 + NX * i:560 + NX * (i + 1)] for i in range(8)]
        tile_e = rows[0:1, 820:820 + 2 * FT]
        tile_ei = rows[0:1, 940:940 + 3 * FT].bitcast(I32)
        M = w_gnn[:, 0:NX * NBLK]
        R1 = w_gnn[:, NX * NBLK:2 * NX * NBLK]
        R2 = w_gnn[:, 2 * NX * NBLK:3 * NX * NBLK]
        R3 = w_gnn[0:1, 0:FT * (NX - 1)]
        xt2, xT2, y2 = (X[:, i * 2 * D:(i + 1) * 2 * D].rearrange("p (s w) -> p s w", s=2) for i in range(3))
        h2 = X[:, 6 * D:6 * D + 2 * NH].rearrange("p (s w) -> p s w", s=2)
        hT2 = X[:, 7 * D:7 * D + 2 * P].rearrange("p (s w) -> p s w", s=2)
        yg = X[:, 8 * D:12 * D].rearrange("p (s w) -> p s w", s=4)

        ps = [ctx.enter_context(nc.psum_tensor(f"ps{i}", [P, 1024], F32)) for i in range(4)]

        x_in, keys_in, next_in, w_in = sem("x_in"), sem("keys_in"), sem("next_in"), sem("w_in")
        const_ready = sem("const_ready")
        meta_id = sem("meta_id")
        v_step = sem("v_step")
        std_ready, var_ready = sem("std_ready"), sem("var_ready")
        h_ready, h_out = sem("h_ready"), sem("h_out")
        stats_done = sem("stats_done")
        init_out = sem("init_out")
        xs_init = sem("xs_init")
        cmp_done = [sem(f"cmp_done{d}") for d in range(2)]
        base_ready = [sem(f"base_ready{d}") for d in range(2)]
        scan_done = [sem(f"scan_done{d}") for d in range(2)]
        masked = [sem(f"masked{d}") for d in range(2)]
        pick_done = [sem(f"pick_done{d}") for d in range(2)]
        slots_ready = [sem(f"slots_ready{d}") for d in range(2)]
        meta_ready = sem("meta_ready")
        linear_out = sem("linear_out")
        from_out, to_out, tables_done = sem("from_out"), sem("to_out"), sem("tables_done")
        disorder_ready, disorder_sum = sem("disorder_ready"), sem("disorder_sum")
        tb_done, td_done, te_done = sem("tb_done"), sem("td_done"), sem("te_done")
        flag_ready = sem("flag_ready")
        table_in = sem("table_in")
        wsum_ready, wt_ready, wt_read = sem("wsum_ready"), sem("wt_ready"), sem("wt_read")
        meta_in = [sem(f"meta_in{u}") for u in range(UNROLL)]
        late_done = [sem(f"late_done{u}") for u in range(UNROLL)]
        key_ready = [sem(f"key_ready{u}") for u in range(UNROLL)]
        idx_ready = [sem(f"idx_ready{h}") for h in range(2)]
        edges_in = [sem(f"edges_in{u}") for u in range(UNROLL)]
        got = [[sem(f"got_{d}_{u}") for u in range(UNROLL)] for d in range(2)]
        rhs_ready = [[sem(f"rhs_ready_{d}_{u}") for u in range(UNROLL)] for d in range(2)]
        mm_done = [[sem(f"mm_done_{d}_{u}") for u in range(UNROLL)] for d in range(2)]
        summed = [sem(f"summed_{d}") for d in range(2)]
        loop_done = sem("loop_done")
        rows_in = sem("rows_in")
        staged, sT_ready, st_copied = sem("staged"), [sem(f"sT_ready{d}") for d in range(2)], [sem(f"st_copied{d}") for d in range(2)]
        agg_ready, agg_read, hx_in = sem("agg_ready"), sem("agg_read"), sem("hx_in")
        rwT_ready, rwT_copied = sem("rwT_ready"), sem("rwT_copied")
        a_step, block_done, x1_done = sem("a_step"), sem("block_done"), sem("x1_done")
        res_done, x1_stat, lg_done, mx_done = sem("res_done"), sem("x1_stat"), sem("lg_done"), sem("mx_done")
        xn_staged, xT_ready, xT_copied, logits_ready = sem("xn_staged"), sem("xT_ready"), sem("xT_copied"), sem("logits_ready")
        picked, r_step = sem("picked"), sem("r_step")
        ffw_in = sem("ffw_in")
        onehot_ready, ranks_ready = sem("onehot_ready"), sem("ranks_ready")
        slots_x_ready, xs_out = sem("slots_x_ready"), sem("xs_out")
        xt_in = [sem(f"xt_in{s}") for s in range(2)]
        f_xT, f_xTc, f_h, f_hc, f_hT, f_hTc, f_o, f_oc = (
            [sem(f"{n}{s}") for s in range(2)]
            for n in ("f_xT", "f_xTc", "f_h", "f_hc", "f_hT", "f_hTc", "f_o", "f_oc"))
        ys_out = [sem(f"ys_out{s}") for s in range(2)]
        tiles_known = sem("tiles_known")
        ones_row = sem("ones_row")
        y_in = [sem(f"y_in{s}") for s in range(4)]
        out_ready = [sem(f"out_ready{s}") for s in range(4)]
        out_done = [sem(f"out_done{s}") for s in range(4)]

        tot_ps = [ps[d][:, 0:NBLK] for d in range(2)]
        base_ps = [ps[d][:, 512:512 + NBLK] for d in range(2)]
        dis_ps = ps[2][:, 512:513]

        block = ctx.enter_context(nc.Block())

        @block.sync
        def _(sp):
            for i, k in ((FROM, src), (TO, dst)):
                sp.dma_start(keys[0:RP, i * RC:(i + 1) * RC],
                             k.rearrange("(p c) -> p c", c=RC)).then_inc(keys_in, 16)
            sp.wait_ge(const_ready, 13)
            xs = x_sb.rearrange("p (b d) -> p b d", b=NBLK)
            sp.dma_start(xs[:, 0:NBLK - 1, :],
                         x[0:(NBLK - 1) * P, :].rearrange("(b p) d -> p b d", p=P)).then_inc(x_in, 16)
            sp.dma_start(xs[0:TAIL, NBLK - 1, :], x[(NBLK - 1) * P:N, :]).then_inc(x_in, 16)
            sp.dma_start(from_dram.rearrange("(p t) f -> p (t f)", p=P), t_init).then_inc(init_out, 16)
            sp.dma_start(to_dram[0:SLOTS, :].rearrange("(p t) f -> p (t f)", p=P), to_init).then_inc(init_out, 16)
            last = (RP - 1) * RC
            sp.dma_start(next_i[0:RP - 1, :], dst[1:last + 1].rearrange("(p c) -> p c", c=RC)).then_inc(next_in, 16)
            sp.dma_start(next_i[RP - 1:RP, 0:RC - 1],
                         dst[last + 1:E].rearrange("(a c) -> a c", a=1)).then_inc(next_in, 16)
            wr = w_raw.rearrange("p (d o i) -> p d o i", d=2, o=2)
            for i, w in ((TO, w_fwd), (FROM, w_back)):
                sp.dma_start(wr[:, i], w.rearrange("(o p) i -> p o i", p=P)).then_inc(w_in, 16)
            sp.wait_ge(meta_ready, 1)
            sp.wait_ge(meta_id, 2)
            sp.dma_start(to_dram[SLOTS:SLOTS + E, :].rearrange("(p c) f -> p (c f)", p=RP),
                         meta[0:RP, TO * RC * 3:(TO + 1) * RC * 3]).then_inc(linear_out, 16)
            sp.wait_ge(h_ready, 1)
            sp.dma_start(h_dram.rearrange("(b p) d -> p b d", p=P),
                         h_sb.rearrange("p (b d) -> p b d", b=NBLK)).then_inc(h_out, 16)
            for c in range(D // P):
                sp.dma_start(xs_dram[:, c * P:(c + 1) * P].rearrange("(a p) w -> p a w", p=P),
                             ones_m[:, :].rearrange("p (a w) -> p a w", a=1).broadcast_to([P, FT, P])).then_inc(xs_init, 16)
            sp.wait_ge(tables_done, 1)
            sp.dma_start(table[:, :], from_dram.rearrange("(p t) f -> p (t f)", p=P)).then_inc(table_in, 16)
            sp.wait_ge(wt_read, 6)
            sp.wait_ge(flag_ready, 1)
            sp.wait_ge(linear_out, 16)

            def load_tiles(k1, with_edges):
                k = k1 - 1
                _, row = nc.values_load_multi_w_load_instructions(
                    tile_rows_i[0:1, bass.ds(k * 2 * UNROLL, 2 * UNROLL)], engines=[mybir.EngineType.SP],
                    min_val=0, max_val=SLOTS + E - P,
                    skip_runtime_bounds_check_because="clamped to the tables when computed")
                for u in range(UNROLL):
                    sp.wait_ge(mm_done[TO][u], k1)
                    sp.dma_start(RG[:, u, :], to_dram[bass.ds(row[2 * u + 1], P), :]).then_inc(meta_in[u], 16)
                    if with_edges:
                        e0 = nc.s_assert_within(row[2 * u], 0, E - P, skip_runtime_bounds_check_because="clamped "
                                                "to the edges when computed")
                        sp.dma_start(Xv[:, TO, u, D:2 * D], edge[bass.ds(e0, P), :]).then_inc(edges_in[u], 16)

            sorted_reg = nc.values_load(flag_i[0:1, 0:1], engines=[mybir.EngineType.SP], min_val=0, max_val=1,
                                        skip_runtime_bounds_check_because="a comparison's 0 or 1")
            with sp.If(sorted_reg == 1):
                with sp.Fori(1, GROUPS + 1) as k1:
                    load_tiles(k1, True)
            with sp.If(sorted_reg == 0):
                with sp.Fori(1, GROUPS + 1) as k1:
                    load_tiles(k1, False)

            sp.wait_ge(loop_done, 1)
            for r, v in ((bf_r, b_fwd), (bb_r, b_back), (ga_r, gamma), (be_r, beta), (rb_r, router_b)):
                sp.dma_start(r, v.rearrange("(a n) -> a n", a=1).broadcast_to([P, v.shape[0]])).then_inc(rows_in, 16)
            sp.dma_start(rw_raw, router_w[:, :]).then_inc(rows_in, 16)

            def weights():
                sp.wait_ge(block_done, NX // 2)
                w1_v = w1.rearrange("(c e) (k p) h -> p c e k h", e=2, p=P)
                w2_v = w2.rearrange("(c e) h n -> h c e n", e=2)
                b2_v = b2.rearrange("(a c e) n -> a c e n", a=1, e=2)
                b1_v = b1.rearrange("(a c e) n -> a c e n", a=1, e=2)
                for e in range(2):
                    at_e = W_AT + e * W_LEN
                    for k in range(2):
                        sp.dma_start(S[:, 0:NX // 2, at_e + k * NH:at_e + (k + 1) * NH],
                                     w1_v[:, :, e, k, :]).then_inc(ffw_in, 16)
                    sp.dma_start(S[0:NH, 0:NX // 2, at_e + 2 * NH:at_e + W_LEN], w2_v[:, :, e, :]).then_inc(ffw_in, 16)
                    sp.dma_start(S[NH:NH + 1, 0:NX // 2, at_e + 2 * NH:at_e + W_LEN],
                                 b2_v[:, :, e, :]).then_inc(ffw_in, 16)
                    sp.dma_start(S[0:1, 0:NX // 2, B1_AT + e * NH:B1_AT + (e + 1) * NH],
                                 b1_v[:, :, e, :]).then_inc(ffw_in, 16)

            with sp.Fori(1, NBLK) as b1_:
                b = b1_ - 1
                sp.wait_ge(x1_done, b1_)
                sp.dma_start(v_h, h_dram[bass.ds(b * P, P), :]).then_inc(hx_in, 16)
                sp.dma_start(xin, x[bass.ds(b * P, P), :]).then_inc(hx_in, 16)
            sp.wait_ge(x1_done, NBLK)
            sp.dma_start(v_h, h_dram[(NBLK - 1) * P:NBLK * P, :]).then_inc(hx_in, 16)
            sp.dma_start(xin[0:TAIL, :], x[(NBLK - 1) * P:N, :]).then_inc(hx_in, 16)
            weights()
            sp.wait_ge(xs_out, 16 * NBLK)
            with sp.Fori(1, FT // 2 + 1) as k1:
                k = k1 - 1
                for s in range(2):
                    sp.wait_ge(f_xT[s], k1)
                    sp.dma_start(xt2[:, s, :], xs_dram[bass.ds((2 * k + s) * P, P), :]).then_inc(xt_in[s], 16)
            for b in range(NBLK):
                n = P if b < NBLK - 1 else TAIL
                sp.wait_ge(out_ready[b % 4], b // 4 + 1)
                sp.dma_start(out[b * P:b * P + n, :], yg[0:n, b % 4, :]).then_inc(out_done[b % 4], 16)
            for s in range(4):
                sp.wait_ge(out_done[s], 16 * len(range(s, NBLK, 4)))

        @block.gpsimd
        def _(g):
            g.memset(x_sb.rearrange("p (b d) -> p b d", b=NBLK)[:, NBLK - 1, :], 0.0).then_inc(const_ready, 1)
            g.memset(next_i, 1 << 24).then_inc(const_ready, 1)
            g.iota(iota_f[:, :], pattern=[[1, P]], base=0, channel_multiplier=0,
                   allow_small_or_imprecise_dtypes=True).then_inc(const_ready, 1)
            g.iota(tile_n, pattern=[[1, TILES]], base=0, channel_multiplier=0,
                   allow_small_or_imprecise_dtypes=True).then_inc(const_ready, 1)
            g.memset(ident[:, :], 0.0).then_inc(const_ready, 1)
            g.memset(before[:, :], 1.0).then_inc(const_ready, 1)
            g.memset(ones_m[:, :], 1.0).then_inc(const_ready, 1)
            g.memset(ones_r, 1.0).then_inc(const_ready, 1)
            g.memset(PRv[:, :, :, D:D + 1], 1.0).then_inc(const_ready, 1)
            for t, f in ((t_init, 0), (to_init, 0)):
                tv = t.rearrange("p (t f) -> p t f", f=3)
                g.memset(tv[:, :, 0:2], 0).then_inc(const_ready, 1)
                g.memset(tv[:, :, 2:3].bitcast(F32), NONE).then_inc(const_ready, 1)
            g.wait_ge(const_ready, 13)
            g.affine_select(out=ident[:, :], in_=ident[:, :], compare_op=ALU.not_equal, fill=1.0, base=0,
                            pattern=[[-1, P]], channel_multiplier=1).then_inc(const_ready, 1)
            g.affine_select(out=before[:, :], in_=before[:, :], compare_op=ALU.is_gt, fill=0.0, base=0,
                            pattern=[[1, P]], channel_multiplier=-1).then_inc(const_ready, 1)
            mt = meta.rearrange("p (d c f) -> p d c f", d=2, f=3)
            for d in range(2):
                g.iota(mt[0:RP, d, :, 0], pattern=[[1, RC]], base=0, channel_multiplier=RC).then_inc(meta_id, 1)
            g.wait_ge(init_out, 32)
            g.wait_ge(meta_id, 2)
            g.wait_ge(slots_ready[FROM], 1)

            def scatter(d, dram_t, done):
                for c in range(RC):
                    g.indirect_dma_start(
                        out=dram_t, out_offset=bass.IndirectOffsetOnAxis(
                            ap=slot_id[0:RP, d * RC + c:d * RC + c + 1], axis=0),
                        in_=mt[0:RP, d, c, :], in_offset=None).then_inc(done, 16)
                g.wait_ge(done, 16 * RC)

            scatter(FROM, from_dram[:, :], from_out)
            g.wait_ge(flag_ready, 1)
            g.wait_ge(slots_ready[TO], 1)
            sorted_reg = nc.values_load(flag_i[0:1, 0:1], engines=[mybir.EngineType.Pool], min_val=0, max_val=1,
                                        skip_runtime_bounds_check_because="a comparison's 0 or 1")
            with g.If(sorted_reg == 0):
                scatter(TO, to_dram[:, :], to_out)
            g.wait_ge(h_out, 16)
            g.nop().then_inc(tables_done, 1)
            g.wait_ge(wt_read, 6)

            def gathers(gather_edges):
                with g.Fori(1, GROUPS + 1) as k1:
                    for u in range(UNROLL):
                        g.wait_ge(const_ready, 15)
                        g.wait_ge(key_ready[u], k1)
                        g.wait_ge(mm_done[TO][u], k1)
                        for f, table_rows in ((0, edge), (1, h_dram)):
                            if f or gather_edges:
                                g.indirect_dma_start(
                                    out=Xv[:, TO, u, (1 - f) * D:(2 - f) * D], out_offset=None,
                                    in_=table_rows[:, :], in_offset=bass.IndirectOffsetOnAxis(
                                        ap=RG[:, u, f:f + 1], axis=0)).then_inc((edges_in, got[TO])[f][u], 16)
                        g.wait_ge(const_ready, 15)
                        if u % 2 == 0:
                            g.wait_ge(idx_ready[u // 2], k1)
                        g.wait_ge(mm_done[FROM][u], k1)
                        for f, table_rows in ((0, edge), (1, h_dram)):
                            g.indirect_dma_start(
                                out=Xv[:, FROM, u, (1 - f) * D:(2 - f) * D], out_offset=None,
                                in_=table_rows[:, :], in_offset=bass.IndirectOffsetOnAxis(
                                    ap=IDv[:, u // 2, u % 2, f:f + 1], axis=0)).then_inc(got[FROM][u], 16)

            with g.If(sorted_reg == 1):
                gathers(False)
            with g.If(sorted_reg == 0):
                gathers(True)
            g.wait_ge(xs_init, 16 * (D // P))
            g.wait_ge(slots_x_ready, 1)
            for b in range(NBLK):
                n = P if b < NBLK - 1 else TAIL
                g.indirect_dma_start(
                    out=xs_dram[:, :], out_offset=bass.IndirectOffsetOnAxis(ap=slot_xi[0:n, b:b + 1], axis=0),
                    in_=S[0:n, b, D:2 * D], in_offset=None).then_inc(xs_out, 16)
            for s in range(2):
                g.wait_ge(ys_out[s], 16 * (FT // 2))
            for b in range(NBLK):
                n = P if b < NBLK - 1 else TAIL
                if b >= 4:
                    g.wait_ge(out_done[b % 4], 16 * (b // 4))
                g.indirect_dma_start(
                    out=yg[0:n, b % 4, :], out_offset=None, in_=ys_dram[:, :],
                    in_offset=bass.IndirectOffsetOnAxis(ap=slot_xi[0:n, b:b + 1], axis=0)).then_inc(y_in[b % 4], 16)

        @block.scalar
        def _(a):
            a.nop().then_inc(st_copied[0], 1)
            a.wait_ge(var_ready, 1)
            a.activation(sm(1, NBLK), sm(0, NBLK), ACT.Sqrt).then_inc(std_ready, 1)
            for i in range(6):
                a.wait_ge(wt_ready, i + 1)
                a.activation(w_gnn[:, i * 2 * D:(i + 1) * 2 * D], ps[1 + i % 3][:, 0:2 * D], ACT.Copy).then_inc(wt_read, 1)
            tb = table[:, :].rearrange("p (t f) -> p t f", f=3)
            a.wait_ge(table_in, 16)
            a.wait_ge(flag_ready, 1)
            with a.Fori(1, GROUPS + 1) as k1:
                k = k1 - 1
                for u in range(UNROLL):
                    if u % 2 == 0:
                        for w in (u, u + 1):
                            a.wait_ge(mm_done[FROM][w], k1)
                        a.activation(IDv[:, u // 2], tb[:, bass.ds(k * UNROLL + u, 2), 0:2],
                                     ACT.Copy).then_inc(idx_ready[u // 2], 1)
                    a.wait_ge(meta_in[u], 16 * k1)
                    a.activation(late[:, u:u + 1], RG[:, u, 0:1], ACT.Relu, scale=-1.0,
                                 bias=first_e[:, bass.ds(k * UNROLL + u, 1)]).then_inc(late_done[u], 1)
                    a.wait_ge(late_done[u], k1)
                    a.activation(key_to[:, u:u + 1], late[:, u:u + 1], ACT.Identity, scale=-4096.0,
                                 bias=RG[:, u, 2:3].bitcast(F32)).then_inc(key_ready[u], 1)
            a.wait_ge(loop_done, 1)
            with a.Fori(1, NBLK + 1) as b1_:
                b = b1_ - 1
                a.wait_ge(sT_ready[1], b1_)
                a.activation(stage, arena[:, bass.ds(b * SB, SB)], ACT.Copy).then_inc(staged, 1)
                a.wait_ge(sT_ready[0], b1_ + 1)
                a.wait_ge(agg_ready, b1_)
                a.activation(ST[:, 0], ps[0][:, 0:6 * P].rearrange("p (k n) -> p k n", k=6),
                             ACT.Copy).then_inc(st_copied[0], 1)
                for i in range(2):
                    a.wait_ge(var_ready, 2 * b + i + 2)
                    a.activation(sm(3, 1), sm(2, 1), ACT.Sqrt).then_inc(std_ready, 1)
                a.wait_ge(block_done, b1_)
                a.wait_ge(xT_ready, b1_)
                a.activation(xn_c, arena[:, bass.ds(b * SB + D, D)], ACT.Copy).then_inc(xn_staged, 1)
                a.wait_ge(xT_ready, b1_ + 1)
                a.activation(xT, ps[2][:, 512:512 + 2 * P], ACT.Copy).then_inc(xT_copied, 1)
            def evacuate(k1):
                for s in range(2):
                    a.wait_ge(f_xT[s], k1 + 1)
                    a.activation(xT2[:, s, :], ps[2 * s][:, 0:2 * P], ACT.Copy).then_inc(f_xTc[s], 1)
                for s in range(2):
                    a.wait_ge(f_h[s], k1)
                    a.activation(h2[:, s, :], ps[2 * s][:, 512:512 + NH], ACT.Relu).then_inc(f_hc[s], 1)

            def store(k1):
                for s in range(2):
                    a.wait_ge(f_oc[s], k1 + 1)
                    a.dma_start(ys_dram[bass.ds(((k1 - 1) * 2 + s) * P, P), :], y2[:, s, :]).then_inc(ys_out[s], 16)

            evacuate(1)
            with a.Fori(1, FT // 2) as k1:
                evacuate(k1 + 1)
                store(k1)
            store(FT // 2)

        @block.vector
        def _(v):
            steps = [0]

            def done(ins):
                steps[0] += 1
                ins.then_inc(v_step, 1)
                v.wait_ge(v_step, steps[0])

            for d in range(2):
                v.nop().then_inc(summed[d], 2)
                v.nop().then_inc(pick_done[d], 1)
            v.nop().then_inc(st_copied[1], 1)
            v.nop().then_inc(agg_read, 1)
            v.nop().then_inc(x1_done, 1)
            v.nop().then_inc(picked, 1)
            for s in range(2):
                v.nop().then_inc(f_oc[s], 1)
            v.wait_ge(const_ready, 15)
            mt = meta.rearrange("p (d c f) -> p d c f", d=2, f=3)
            tile_f, tend, off = sm(7), sm(14), sm(15)
            cnt = sm(4)
            for d in (FROM, TO):
                kd, bi, li = (t[0:RP, d * RC:(d + 1) * RC] for t in (keys, blk_i, low_i))
                bh = blk_h[0:RP, d * (RC + 1):d * (RC + 1) + RC]
                v.wait_ge(keys_in, 32)
                done(v.tensor_scalar(bi, kd, 7, None, ALU.logical_shift_right))
                done(v.tensor_copy(bh, bi))
                with v.Fori(0, NBLK) as b:
                    v.tensor_scalar(member[0:RP, bass.ds(b * RC, RC)], bh,
                                    iota_f[0:RP, bass.ds(b, 1)], 0.0, ALU.is_equal, ALU.add,
                                    accum_out=cnt[0:RP, bass.ds(b + d * NBLK, 1)]).then_inc(cmp_done[d], 1)
                v.wait_ge(cmp_done[d], NBLK)
                done(v.tensor_copy(mt[0:RP, d, :, 1], keys[0:RP, (1 - d) * RC:(2 - d) * RC]))
                if d == FROM:
                    done(v.tensor_scalar(li, kd, P - 1, None, ALU.bitwise_and))
                    done(v.tensor_copy(mt[0:RP, d, :, 2].bitcast(F32), li))
                else:
                    done(v.tensor_copy(mt[0:RP, d, :, 2].bitcast(F32), kd))
                    v.nop().then_inc(meta_ready, 1)
                c25 = slice(d * NBLK, (d + 1) * NBLK)
                v.wait_ge(base_ready[d], 1)
                done(v.tensor_scalar(sm(5, dt=I32)[:, c25], tot_ps[d], float(P - 1), None, ALU.add))
                done(v.tensor_scalar(sm(6, dt=I32)[:, c25], sm(5, dt=I32)[:, c25], 7, None, ALU.logical_shift_right))
                done(v.tensor_copy(tile_f[:, c25], sm(6, dt=I32)[:, c25]))
                done(v.tensor_tensor_scan(tend[:, c25], ones_m[:, 0:NBLK], tile_f[:, c25], 0.0, ALU.mult, ALU.add))
                done(v.tensor_tensor(tile_f[:, c25], tend[:, c25], tile_f[:, c25], ALU.subtract))
                done(v.tensor_scalar(tile_f[:, c25], tile_f[:, c25], float(P), -1.0, ALU.mult, ALU.add))
                done(v.tensor_tensor(off[0:RP, c25], base_ps[d][0:RP, :], tile_f[0:RP, c25], ALU.add))
                po = pos[0:RP, :]
                done(v.memset(po, 0.0))
                with v.Fori(1, NBLK + 1) as b1_:
                    b = b1_ - 1
                    mem = member[0:RP, bass.ds(b * RC, RC)]
                    rk = rank[0:RP, 0:RC]
                    v.wait_ge(pick_done[d], b1_)
                    v.tensor_tensor_scan(rk, ones_r[0:RP, :], mem, off[0:RP, bass.ds(b + d * NBLK, 1)],
                                         ALU.mult, ALU.add).then_inc(scan_done[d], 1)
                    v.wait_ge(scan_done[d], b1_)
                    v.tensor_tensor(rk, rk, mem, ALU.mult).then_inc(masked[d], 1)
                    v.wait_ge(masked[d], b1_)
                    v.tensor_tensor(po, po, rk, ALU.add).then_inc(pick_done[d], 1)
                v.wait_ge(pick_done[d], NBLK + 1)
                si = slot_id[0:RP, d * RC:(d + 1) * RC]
                if d == TO:
                    done(v.tensor_copy(si, po))
                else:
                    done(v.tensor_copy(pos_i[0:RP, :], po))
                    done(v.tensor_scalar(row_i[0:RP, :], pos_i[0:RP, :], P - 1, None, ALU.bitwise_and))
                    done(v.tensor_scalar(col_i[0:RP, :], pos_i[0:RP, :], 7, None, ALU.logical_shift_right))
                    done(v.scalar_tensor_tensor(si, row_i[0:RP, :], float(TILES), col_i[0:RP, :], ALU.mult, ALU.add))
                v.nop().then_inc(slots_ready[d], 1)

            v.wait_ge(next_in, 32)
            nx = next_i[0:RP, :]
            done(v.tensor_scalar(row_i[0:RP, :], nx, 7, None, ALU.logical_shift_right))
            done(v.tensor_tensor(rank[0:RP, 0:RC], row_i[0:RP, :], blk_i[0:RP, TO * RC:(TO + 1) * RC], ALU.is_lt))
            v.tensor_reduce(sorted_f[0:RP, 0:1], rank[0:RP, 0:RC], AX.X, ALU.add).then_inc(disorder_ready, 1)
            v.wait_ge(disorder_sum, 1)
            done(v.tensor_scalar(sorted_f[:, 1:2], dis_ps, 0.0, None, ALU.is_equal))
            in_order = sorted_f[:, 1:2]
            done(v.tensor_copy(flag_i[0:1, :], in_order[0:1, :]))

            tbv = tile_b.rearrange("p (t d) -> p t d", d=2)
            done(v.memset(tile_b, 0.0))
            done(v.memset(delta_t, 0.0))
            done(v.tensor_tensor_scan(sm(8, NBLK), ones_m[:, 0:NBLK], tot_ps[TO], 0.0, ALU.mult, ALU.add))
            done(v.tensor_tensor(sm(8, NBLK), sm(8, NBLK), tot_ps[TO], ALU.subtract))
            done(v.tensor_tensor(sm(8, NBLK), sm(8, NBLK), tile_f[:, TO * NBLK:(TO + 1) * NBLK], ALU.subtract))
            done(v.tensor_tensor(sm(9, NBLK - 1), sm(8, NBLK)[:, 1:NBLK], sm(8, NBLK)[:, 0:NBLK - 1], ALU.subtract))
            v.nop().then_inc(tb_done, 1)
            v.nop().then_inc(td_done, 1)
            with v.Fori(1, NBLK) as b1_:
                b = b1_ - 1
                v.wait_ge(tb_done, b1_)
                v.scalar_tensor_tensor(tbv[:, :, FROM], tile_n, tend[:, bass.ds(b + FROM * NBLK, 1)],
                                       tbv[:, :, FROM], ALU.is_ge, ALU.add)
                v.scalar_tensor_tensor(tbv[:, :, TO], tile_n, tend[:, bass.ds(b + TO * NBLK, 1)],
                                       tbv[:, :, TO], ALU.is_ge, ALU.add).then_inc(tb_done, 1)
                v.wait_ge(td_done, b1_)
                v.tensor_scalar(step_t, tile_n, tend[:, bass.ds(b + TO * NBLK, 1)], sm(9, NBLK - 1)[:, bass.ds(b, 1)],
                                ALU.is_ge, ALU.mult).then_inc(te_done, 1)
                v.wait_ge(te_done, b1_)
                v.tensor_tensor(delta_t, delta_t, step_t, ALU.add).then_inc(td_done, 1)
            v.wait_ge(tb_done, NBLK)
            v.wait_ge(td_done, NBLK)
            done(v.tensor_copy(tile_blk_i[:, :], tile_b[0:1, :]))
            done(v.tensor_scalar(neg_blk[:, :], tbv[:, :, TO], -float(P), None, ALU.mult))
            done(v.tensor_scalar(step_t, tile_n, float(P), -1.0, ALU.mult, ALU.add))
            done(v.tensor_scalar(delta_t, delta_t, sm(8, NBLK)[:, 0:1], None, ALU.add))
            done(v.tensor_tensor(delta_t, delta_t, step_t, ALU.add))
            done(v.tensor_scalar(first_e[:, :], delta_t, in_order, None, ALU.mult))
            rf = rows_f.rearrange("p (t f) -> p t f", f=2)
            done(v.tensor_scalar(rf[:, :, 0], delta_t, float(E - P), None, ALU.min))
            done(v.tensor_scalar(step_t, tile_n, float(P), None, ALU.mult))
            done(v.tensor_tensor(delta_t, rf[:, :, 0], step_t, ALU.subtract))
            done(v.tensor_scalar(delta_t, delta_t, float(SLOTS), in_order, ALU.add, ALU.mult))
            done(v.tensor_tensor(rf[:, :, 1], delta_t, step_t, ALU.add))
            done(v.tensor_copy(tile_rows_i[:, :], rows_f[0:1, :]))
            v.nop().then_inc(flag_ready, 1)

            v.wait_ge(x_in, 32)
            xs = x_sb.rearrange("p (b d) -> p b d", b=NBLK)
            hs = h_sb.rearrange("p (b d) -> p b d", b=NBLK)
            st6 = sm(10, 6 * NBLK)
            mv = sm(13, 2 * NBLK)
            for b in range(NBLK):
                v.bn_stats(st6[:, 6 * b:6 * b + 6], xs[:, b, :]).then_inc(stats_done, 1)
            v.wait_ge(stats_done, NBLK)
            for b in range(NBLK):
                v.bn_aggr(mv[:, 2 * b:2 * b + 2], st6[:, 6 * b:6 * b + 6]).then_inc(stats_done, 1)
            v.wait_ge(stats_done, 2 * NBLK)
            mv2 = mv.rearrange("p (b t) -> p b t", t=2)
            v.tensor_scalar(sm(0, NBLK), mv2[:, :, 1], EPS, None, ALU.add).then_inc(var_ready, 1)
            v.wait_ge(std_ready, 1)
            done(v.reciprocal(sm(0, NBLK), sm(1, NBLK)))
            for b in range(NBLK):
                v.tensor_scalar(hs[:, b, :], xs[:, b, :], mv2[:, b, 0:1], sm(0, NBLK)[:, b:b + 1],
                                ALU.subtract, ALU.mult).then_inc(stats_done, 1)
            v.wait_ge(stats_done, 3 * NBLK)
            v.nop().then_inc(h_ready, 1)
            v.wait_ge(w_in, 32)
            wr = w_raw.rearrange("p (d o i) -> p (d o) i", d=2, o=2)
            for part in range(2):
                w = wr[:, :, part * D:(part + 1) * D]
                v.tensor_tensor(w, w, wr[:, :, 2 * D:3 * D], ALU.add).then_inc(wsum_ready, 1)
            v.wait_ge(tables_done, 1)
            v.wait_ge(h_out, 16)
            v.wait_ge(init_out, 32)
            v.wait_ge(linear_out, 16)
            done(v.memset(arena[:, :], 0.0))

            v.wait_ge(table_in, 16)
            tbf = table[:, :].bitcast(F32)
            with v.Fori(1, GROUPS + 1) as k1:
                k = k1 - 1
                _, blocks = nc.values_load_multi_w_load_instructions(
                    tile_blk_i[0:1, bass.ds(k * 2 * UNROLL, 2 * UNROLL)], engines=[mybir.EngineType.DVE],
                    min_val=0, max_val=NBLK - 1,
                    skip_runtime_bounds_check_because="a count of at most NBLK - 1 comparisons that hold")

                def operands(u):
                    for d in range(2):
                        if u >= 2:
                            v.wait_ge(mm_done[d][u - 2], k1 + 1)
                        else:
                            v.wait_ge(mm_done[d][u + 2], k1)
                        if d == TO:
                            v.wait_ge(key_ready[u], k1)
                            v.tensor_scalar(OHv[:, d, u % 2, :], iota_f[:, :], key_to[:, u:u + 1],
                                            neg_blk[:, bass.ds(k * UNROLL + u, 1)],
                                            ALU.subtract, ALU.is_equal).then_inc(rhs_ready[d][u], 1)
                        else:
                            v.tensor_scalar(OHv[:, d, u % 2, :], iota_f[:, :],
                                            tbf[:, bass.ds((k * UNROLL + u) * 3 + 2, 1)], None,
                                            ALU.is_equal).then_inc(rhs_ready[d][u], 1)
                        if d == TO:
                            v.wait_ge(got[d][u], 16 * k1)
                            v.wait_ge(edges_in[u], 16 * k1)
                        else:
                            v.wait_ge(got[d][u], 32 * k1)
                        v.tensor_tensor(PRv[:, d, u % 2, 0:D], Xv[:, d, u, 0:D], Xv[:, d, u, D:2 * D],
                                        ALU.mult).then_inc(rhs_ready[d][u], 1)

                def add(u):
                    for d in range(2):
                        sums = arena[:, bass.ds(blocks[2 * u + d] * SB + d * SW, SW)]
                        v.wait_ge(mm_done[d][u], k1 + 1)
                        v.wait_ge(summed[d], k * UNROLL + u + 2)
                        v.tensor_tensor(sums, sums, ps[2 * d + u % 2][:, 0:SW], ALU.add).then_inc(summed[d], 1)

                operands(0)
                for u in range(1, UNROLL):
                    operands(u)
                    add(u - 1)
                add(UNROLL - 1)
            for d in range(2):
                v.wait_ge(summed[d], TILES + 2)
            v.nop().then_inc(loop_done, 1)

            v.wait_ge(rows_in, 16 * 6)
            v.wait_ge(rwT_ready, 1)
            done(v.tensor_copy(rwT, ps[3][:, 512:512 + 2 * NX]))
            v.nop().then_inc(rwT_copied, 1)
            PER = 15

            def project(b, b1_, b2_):
                n = [0]

                def then(ins, own=None):
                    if own is None:
                        n[0] += 1
                        ins.then_inc(a_step, 1)
                        v.wait_ge(a_step, b * PER + n[0])
                    else:
                        ins.then_inc(own, 1)
                        v.wait_ge(const_ready, 15)
                        v.wait_ge(own, b2_ if own is x1_done else b1_)

                v.wait_ge(agg_ready, b1_)
                v.wait_ge(sT_ready[1], b2_)
                v.tensor_copy(ST[:, 1], ps[1][:, 0:6 * P].rearrange("p (k n) -> p k n", k=6)).then_inc(st_copied[1], 1)
                cf = arena[:, bass.ds(b * SB + SW - 1, 1)]
                cb = arena[:, bass.ds(b * SB + 2 * SW - 1, 1)]
                x1 = arena[:, bass.ds(b * SB, D)]
                xn = arena[:, bass.ds(b * SB + D, D)]
                then(v.tensor_tensor(sm(16, 1), cf, cb, ALU.add))
                then(v.tensor_scalar(sm(16, 1), sm(16, 1), 1.0, None, ALU.max))
                then(v.reciprocal(sm(16, 1), sm(16, 1)))
                v.wait_ge(agg_ready, b2_)
                then(v.scalar_tensor_tensor(v_a, bf_r, cf, ps[2][:, 0:D], ALU.mult, ALU.add))
                v.nop().then_inc(agg_read, 1)
                then(v.scalar_tensor_tensor(v_a, bb_r, cb, v_a, ALU.mult, ALU.add))
                then(v.tensor_scalar(v_a, v_a, sm(16, 1), None, ALU.mult))
                then(v.scalar_tensor_tensor(v_a, v_a, SLOPE, v_a, ALU.mult, ALU.max))
                v.wait_ge(hx_in, 32 * b1_)
                then(v.tensor_tensor(v_a, v_a, v_h, ALU.add))
                then(v.bn_stats(sm(17, 6), v_a), res_done)
                then(v.bn_aggr(sm(17, 12)[:, 8:10], sm(17, 6)))
                v.tensor_scalar(sm(2, 1), sm(17, 12)[:, 9:10], EPS, None, ALU.add).then_inc(var_ready, 1)
                v.wait_ge(std_ready, 2 * b + 2)
                then(v.reciprocal(sm(16, 2)[:, 1:2], sm(3, 1)))
                then(v.tensor_scalar(v_a, v_a, sm(17, 12)[:, 8:9], sm(16, 2)[:, 1:2], ALU.subtract, ALU.mult))
                then(v.tensor_tensor(v_a, v_a, ga_r, ALU.mult))
                then(v.tensor_tensor(v_a, v_a, be_r, ALU.add))
                then(v.tensor_tensor(x1, v_a, xin, ALU.add), x1_done)
                then(v.bn_stats(sm(17, 6), x1), x1_stat)
                then(v.bn_aggr(sm(17, 12)[:, 8:10], sm(17, 6)))
                v.tensor_scalar(sm(2, 1), sm(17, 12)[:, 9:10], EPS, None, ALU.add).then_inc(var_ready, 1)
                v.wait_ge(std_ready, 2 * b + 3)
                then(v.reciprocal(sm(16, 2)[:, 1:2], sm(3, 1)))
                v.tensor_scalar(xn, x1, sm(17, 12)[:, 8:9], sm(16, 2)[:, 1:2], ALU.subtract,
                                ALU.mult).then_inc(block_done, 1)
                assert n[0] == PER

            def route(b, b1_):
                v.wait_ge(logits_ready, b1_)
                v.tensor_tensor(lg, ps[3][:, 0:NX], rb_r, ALU.add).then_inc(lg_done, 1)
                v.wait_ge(const_ready, 15)
                v.wait_ge(lg_done, b1_)
                v.max(mx8, lg).then_inc(mx_done, 1)
                v.wait_ge(const_ready, 15)
                v.wait_ge(mx_done, b1_)
                v.max_index(mi8, mx8, lg).then_inc(r_step, 1)
                v.wait_ge(r_step, b1_)
                v.tensor_copy(eid[:, bass.ds(b, 1)], mi8[:, 0:1]).then_inc(picked, 1)

            project(0, 1, 2)
            with v.Fori(1, NBLK) as b:
                b2_ = v.snap(b + 2)
                b1_ = v.snap(b + 1)
                project(b, b1_, b2_)
                route(b - 1, b)
            route(NBLK - 1, NBLK)
            v.wait_ge(picked, NBLK + 1)

            Mv = M.rearrange("p (e b) -> p e b", e=NX)
            ib = iota_f[:, 0:NX].rearrange("p (e a) -> p e a", a=1).broadcast_to([P, NX, NBLK])
            eb = eid.rearrange("p (a b) -> p a b", a=1).broadcast_to([P, NX, NBLK])
            done(v.tensor_tensor(Mv, ib, eb, ALU.is_equal))
            done(v.tensor_reduce(valid, ident[:, 0:TAIL], AX.X, ALU.add))
            done(v.tensor_scalar(Mv[:, :, NBLK - 1], Mv[:, :, NBLK - 1], valid, None, ALU.mult))
            v.nop().then_inc(onehot_ready, 1)
            v.wait_ge(ranks_ready, 1)
            rk_ps, ct_ps = ps[0][:, 0:NX * NBLK], ps[1][:, 0:NX * NBLK]
            half = NX * NBLK // 2
            rk_ps = [ps[0][:, 0:half], ps[0][:, 512:512 + half]]
            ct_ps = [ps[1][:, 0:half], ps[1][:, 512:512 + half]]
            for i in range(2):
                done(v.tensor_copy(R1[:, i * half:(i + 1) * half], ct_ps[i]))
            one = ones_m[:, 0:1].broadcast_to([P, NX * NBLK])
            done(v.tensor_tensor_scan(R2, one, R1, 0.0, ALU.mult, ALU.add))
            ex_c, ex_i, ex_t, ex_e, ex_s, ex_p = ex[0], ex[1].bitcast(I32), ex[2], ex[3], ex[4], ex[5]
            done(v.tensor_reduce(ex_c, R1.rearrange("p (e b) -> p e b", e=NX), AX.X, ALU.add))
            done(v.tensor_scalar(ex_i, ex_c, float(P - 1), None, ALU.add))
            done(v.tensor_scalar(ex_s.bitcast(I32), ex_i, 7, None, ALU.logical_shift_right))
            done(v.tensor_copy(ex_t, ex_s.bitcast(I32)))
            done(v.tensor_tensor_scan(ex_e, ones_m[:, 0:NX], ex_t, 0.0, ALU.mult, ALU.add))
            done(v.tensor_tensor(ex_t, ex_e, ex_t, ALU.subtract))
            done(v.tensor_tensor_scan(ex_s, ones_m[:, 0:NX], ex_c, 0.0, ALU.mult, ALU.add))
            done(v.tensor_tensor(ex_s, ex_s, ex_c, ALU.subtract))
            done(v.scalar_tensor_tensor(ex_p, ex_t, float(P), ex_s, ALU.mult, ALU.subtract))
            done(v.tensor_tensor(R2, R2, R1, ALU.subtract))
            for i in range(2):
                part = R2[:, i * half:(i + 1) * half]
                done(v.tensor_tensor(part, part, rk_ps[i], ALU.add))
            R2v = R2.rearrange("p (e b) -> p e b", e=NX)
            done(v.tensor_tensor(R2v, R2v, ex_p.rearrange("p (e a) -> p e a", a=1).broadcast_to([P, NX, NBLK]), ALU.add))
            done(v.tensor_tensor(R2, R2, M, ALU.mult))
            done(v.tensor_reduce(slot_x, R2.rearrange("p (e b) -> p b e", e=NX), AX.X, ALU.add))
            done(v.tensor_copy(slot_xi, slot_x))
            v.nop().then_inc(slots_x_ready, 1)
            tv = R3.rearrange("p (t e) -> p t e", e=NX - 1)
            done(v.tensor_tensor(tv, iota_f[0:1, 0:FT].rearrange("p (t a) -> p t a", a=1).broadcast_to([1, FT, NX - 1]),
                                 ex_e[0:1, 0:NX - 1].rearrange("p (a e) -> p a e", a=1).broadcast_to([1, FT, NX - 1]),
                                 ALU.is_ge))
            te = tile_e[:, 0:FT]
            done(v.tensor_reduce(te, tv, AX.X, ALU.add))
            ti = tile_ei.rearrange("p (f t) -> p f t", f=3)
            done(v.tensor_copy(ti[:, 0, :], te))
            done(v.tensor_scalar(ti[:, 1, :], ti[:, 0, :], 1, None, ALU.logical_shift_right))
            done(v.tensor_scalar(ti[:, 2, :], ti[:, 0, :], 1, None, ALU.bitwise_and))
            done(v.tensor_scalar(te, ti[:, 1, :], float(SB), None, ALU.mult))
            tp = ti.rearrange("p f t -> p (f t)")[:, 0:2 * FT].rearrange("p (t f) -> p t f", f=2)
            ww = tile_e.rearrange("p (f t) -> p f t", f=2)[:, 1, :]
            done(v.scalar_tensor_tensor(ww, ti[:, 2, :], float(W_LEN), te, ALU.mult, ALU.add))
            done(v.scalar_tensor_tensor(te, ti[:, 2, :], float(NH), te, ALU.mult, ALU.add))
            done(v.tensor_copy(tp[:, :, 0], ww))
            done(v.tensor_copy(tp[:, :, 1], te))
            v.nop().then_inc(tiles_known, 1)

            done(v.memset(hT2[NH:NH + 1, :, :], 1.0))
            v.nop().then_inc(ones_row, 1)

            def expert_tiles(k1):
                for s in range(2):
                    v.wait_ge(f_hT[s], k1)
                    v.tensor_copy(hT2[0:NH, s, :], ps[2 * s + 1][0:NH, 0:P]).then_inc(f_hTc[s], 1)
                for s in range(2):
                    v.wait_ge(f_o[s], k1)
                    if not isinstance(k1, int):
                        v.wait_ge(ys_out[s], 16 * (k1 - 1))
                    v.tensor_scalar(y2[:, s, :], ps[2 * s + 1][:, 512:512 + D], 0.0, None, ALU.max).then_inc(f_oc[s], 1)

            expert_tiles(1)
            with v.Fori(2, FT // 2 + 1) as k1:
                expert_tiles(k1)
            for b in range(NBLK):
                n = P if b < NBLK - 1 else TAIL
                v.wait_ge(y_in[b % 4], 16 * (b // 4 + 1))
                y = yg[0:n, b % 4, :]
                v.tensor_tensor(y, y, S[0:n, b, 0:D], ALU.add).then_inc(out_ready[b % 4], 1)

        @block.tensor
        def _(pe):
            for d in range(2):
                for u in range(UNROLL):
                    pe.nop().then_inc(mm_done[d][u], 1)
            pe.nop().then_inc(sT_ready[0], 1)
            pe.nop().then_inc(sT_ready[1], 1)
            pe.nop().then_inc(agg_ready, 1)
            pe.nop().then_inc(xT_ready, 1)
            for s in range(2):
                pe.nop().then_inc(f_xT[s], 1)
            cnt = sm(4)
            pe.wait_ge(const_ready, 15)
            for d in (FROM, TO):
                pe.wait_ge(cmp_done[d], NBLK)
                nc.tensor.matmul(tot_ps[d], ones_m[0:RP, :], cnt[0:RP, d * NBLK:(d + 1) * NBLK], start=True, stop=True)
                nc.tensor.matmul(base_ps[d], before[0:RP, :], cnt[0:RP, d * NBLK:(d + 1) * NBLK],
                                 start=True, stop=True).then_inc(base_ready[d], 1)
            pe.wait_ge(disorder_ready, 1)
            nc.tensor.matmul(dis_ps, ones_m[0:RP, :], sorted_f[0:RP, 0:1], start=True, stop=True).then_inc(disorder_sum, 1)
            pe.wait_ge(wsum_ready, 2)
            pe.wait_ge(flag_ready, 1)
            ws = w_raw.rearrange("p (d o i) -> p d o i", d=2, o=2)
            for i in range(6):
                if i >= 3:
                    pe.wait_ge(wt_read, i - 2)
                for j in range(2):
                    d, kk = (2 * i + j) // 6, (2 * i + j) % 6
                    col = kk * P if kk < 4 else (kk + 2) * P
                    for o in range(2):
                        last = nc.tensor.transpose(ps[1 + i % 3][:, (2 * j + o) * P:(2 * j + o + 1) * P],
                                                   ws[:, d, o, col:col + P], ident[:, :])
                last.then_inc(wt_ready, 1)
            pe.wait_ge(wt_read, 6)
            with pe.Fori(1, GROUPS + 1) as k1:
                k = k1 - 1
                for u in range(UNROLL):
                    for d in range(2):
                        pe.wait_ge(rhs_ready[d][u], 2 * k1)
                        pe.wait_ge(summed[d], k * UNROLL + u + 1)
                        acc = ps[2 * d + u % 2]
                        nc.tensor.matmul(acc[:, 0:512], OHv[:, d, u % 2, :], Xv[:, d, u, :], start=True, stop=True)
                        nc.tensor.matmul(acc[:, 512:SW], OHv[:, d, u % 2, :], PRv[:, d, u % 2, :], start=True,
                                         stop=True).then_inc(mm_done[d][u], 1)
            pe.wait_ge(loop_done, 1)
            pe.wait_ge(rows_in, 16 * 6)
            for kk in range(2):
                last = nc.tensor.transpose(ps[3][:, 512 + kk * NX:512 + (kk + 1) * NX],
                                           rw_raw[:, kk * P:(kk + 1) * P], ident[0:NX, 0:NX])
            last.then_inc(rwT_ready, 1)
            pe.wait_ge(rwT_copied, 1)
            with pe.Fori(1, NBLK + 1) as b1_:
                pe.wait_ge(staged, b1_)
                for d in range(2):
                    pe.wait_ge(st_copied[d], b1_)
                    for kk in range(6):
                        last = nc.tensor.transpose(ps[d][:, kk * P:(kk + 1) * P],
                                                   stage[:, d * SW + kk * P:d * SW + (kk + 1) * P], ident[:, :])
                    last.then_inc(sT_ready[d], 1)
                pe.wait_ge(agg_read, b1_)
                for d in range(2):
                    pe.wait_ge(st_copied[d], b1_ + 1)
                    for kk in range(6):
                        last = nc.tensor.matmul(ps[2][:, 0:D], ST[:, d, kk, :],
                                                w_gnn[:, (d * 6 + kk) * D:(d * 6 + kk + 1) * D],
                                                start=(d == 0 and kk == 0), stop=(d == 1 and kk == 5))
                last.then_inc(agg_ready, 1)
                pe.wait_ge(xn_staged, b1_)
                for kk in range(2):
                    last = nc.tensor.transpose(ps[2][:, 512 + kk * P:512 + (kk + 1) * P],
                                               xn_c[:, kk * P:(kk + 1) * P], ident[:, :])
                last.then_inc(xT_ready, 1)
                pe.wait_ge(xT_copied, b1_)
                pe.wait_ge(picked, b1_)
                for kk in range(2):
                    last = nc.tensor.matmul(ps[3][:, 0:NX], xT[:, kk * P:(kk + 1) * P],
                                            rwT[:, kk * NX:(kk + 1) * NX], start=(kk == 0), stop=(kk == 1))
                last.then_inc(logits_ready, 1)
            pe.wait_ge(onehot_ready, 1)
            half = NX * NBLK // 2
            for i in range(2):
                nc.tensor.matmul(ps[0][:, i * 512:i * 512 + half], before[:, :], M[:, i * half:(i + 1) * half],
                                 start=True, stop=True)
                last = nc.tensor.matmul(ps[1][:, i * 512:i * 512 + half], ones_m[:, :], M[:, i * half:(i + 1) * half],
                                        start=True, stop=True)
            last.then_inc(ranks_ready, 1)
            pe.wait_ge(tiles_known, 1)
            pe.wait_ge(ones_row, 1)
            pe.wait_ge(ffw_in, 16 * 10)
            with pe.Fori(1, FT // 2 + 1) as k1:
                k = k1 - 1
                _, at_ = nc.values_load_multi_w_load_instructions(
                    tile_ei[0:1, bass.ds(k * 4, 4)], engines=[mybir.EngineType.PE],
                    min_val=0, max_val=(NX // 2 - 1) * SB + W_LEN,
                    skip_runtime_bounds_check_because="a count of at most NX - 1 comparisons, scaled")
                for s in range(2):
                    pe.wait_ge(xt_in[s], 16 * k1)
                    for kk in range(2):
                        last = nc.tensor.transpose(ps[2 * s][:, kk * P:(kk + 1) * P],
                                                   xt2[:, s, kk * P:(kk + 1) * P], ident[:, :])
                    last.then_inc(f_xT[s], 1)
                for s in range(2):
                    pe.wait_ge(f_xTc[s], k1)
                    h = ps[2 * s][:, 512:512 + NH]
                    nc.tensor.matmul(h, ones_m[0:1, :], arena[0:1, bass.ds(at_[2 * s + 1] + B1_AT, NH)],
                                     start=True, stop=False)
                    for kk in range(2):
                        last = nc.tensor.matmul(h, xT2[:, s, kk * P:(kk + 1) * P],
                                                arena[:, bass.ds(at_[2 * s] + W_AT + kk * NH, NH)],
                                                start=False, stop=(kk == 1))
                    last.then_inc(f_h[s], 1)
                for s in range(2):
                    pe.wait_ge(const_ready, 15)
                    pe.wait_ge(f_hc[s], k1)
                    nc.tensor.transpose(ps[2 * s + 1][0:NH, 0:P], h2[:, s, :], ident[:, :]).then_inc(f_hT[s], 1)
                for s in range(2):
                    pe.wait_ge(f_hTc[s], k1)
                    pe.wait_ge(f_oc[s], k1)
                    nc.tensor.matmul(ps[2 * s + 1][:, 512:512 + D], hT2[0:NH + 1, s, :],
                                     arena[0:NH + 1, bass.ds(at_[2 * s] + W_AT + 2 * NH, D)],
                                     start=True, stop=True).then_inc(f_o[s], 1)


_INS = ['x', 'src', 'dst', 'edge_attr_256', 'L0_gnn_W_fwd', 'L0_gnn_b_fwd', 'L0_gnn_W_back', 'L0_gnn_b_back',
        'L0_gnn_gamma', 'L0_gnn_beta', 'L0_ffn_router_w', 'L0_ffn_router_b', 'L0_ffn_W1', 'L0_ffn_b1',
        'L0_ffn_W2', 'L0_ffn_b2']


def kernel(**inputs):
    import numpy as _np
    import concourse.bacc as _bacc
    from concourse import mybir as _mybir
    from concourse.bass_utils import run_bass_kernel_spmd as _run

    nc = _bacc.Bacc("TRN2", target_bir_lowering=False, num_devices=1)
    arrays, args = {}, []
    for name in _INS:
        a = _np.ascontiguousarray(inputs[name])
        arrays[f"in_{name}_dram"] = a
        args.append(nc.dram_tensor(f"in_{name}_dram", a.shape, _mybir.dt.from_np(a.dtype), kind="ExternalInput").ap())
    out = nc.dram_tensor("out_0_dram", (N, D), _mybir.dt.float32, kind="ExternalOutput").ap()
    gnn_ffn(nc, *args, out)
    r = _run(nc, [arrays], core_ids=[0])
    return r.results[0]["out_0_dram"]
```

```python
import concourse.bass as bass
from concourse import mybir
from contextlib import ExitStack

F32, I32, U16, BF16 = mybir.dt.float32, mybir.dt.int32, mybir.dt.uint16, mybir.dt.bfloat16
ALU = mybir.AluOpType
ACT = mybir.ActivationFunctionType
AX = mybir.AxisListType

P = 128
N, D = 3125, 256
E = 53125
RP, RC = 125, 425
NBLK = (N + P - 1) // P
TAIL = N - (NBLK - 1) * P
UNROLL = 8
RANKS = 5
RING = 4
TILES = -(-((E + NBLK * (P - 1)) // P) // UNROLL) * UNROLL
GROUPS = TILES // UNROLL
SLOTS = P * TILES
SW = 3 * D + 1
SB = 2 * SW
NX, NH, SLOPE, EPS = 32, 64, 0.01, 1e-5
FT = (N + NX * (P - 1)) // P
ES = 4
W_AT = 2 * D
W_LEN = 2 * NH + D
B1_AT = W_AT + 2 * W_LEN
NONE = -1048576.0
FULL = E // P
XS = 2 * D + 6
DST, KEY, EDGE, SRC, SLOT, NDST = range(6)
SENT = D + 2
TO, FROM = 0, 1


def gnn_ffn(nc, x, src, dst, edge, w_fwd, b_fwd, w_back, b_back, gamma, beta,
            router_w, router_b, w1, b1, w2, b2, out):
    assert RP * RC == E and FT % ES == 0 and B1_AT + 2 * NH <= SB and NX // 2 <= NBLK
    assert NBLK % RANKS == 0
    ctx = ExitStack()
    with ctx:
        def sb(name, cols, dt=F32, rows=P):
            return ctx.enter_context(nc.sbuf_tensor(name, [rows, cols], dt))

        def sem(name):
            return ctx.enter_context(nc.semaphore(name))

        def dram(name, shape, dt=F32):
            return nc.dram_tensor(name, shape, dt, kind="Internal").ap()

        h_dram = dram("h_rows", (NBLK * P, D))
        to_dram = dram("to_table", (SLOTS + E, 6), I32)
        from_dram = dram("rows_by_src", (SLOTS, SENT))
        xs_dram = dram("rows_by_expert", (FT * P, D))
        ys_dram = dram("outputs_by_expert", (FT * P, D))

        arena = sb("arena", NBLK * SB)
        at = [0]

        def carve(cols, dt=F32):
            words = cols if dt in (F32, I32) else (cols + 1) // 2
            assert at[0] + words <= NBLK * SB
            a = at[0]
            at[0] = a + words
            assert at[0] <= NBLK * SB
            v = arena[:, a:a + words]
            return v if dt == F32 else v.bitcast(dt)

        x_sb = carve(NBLK * D)
        h_sb = carve(NBLK * D)
        NODES_END = at[0]
        keys = carve(2 * RC, I32)
        next_i = carve(RC, I32)
        blk_i = carve(2 * RC, I32)
        low_i = carve(RC, I32)
        blk_h = carve(2 * (RC + 1), BF16)
        ones_r = carve(RC)
        rank = carve(RANKS * RC)
        pos = carve(RC)
        row_i = carve(RC, I32)
        member = carve(NBLK * RC, U16)
        to_init = carve(TILES * 6, I32)
        empty = carve(SENT)
        EDGES_END = at[0]
        tile_n = carve(TILES)
        tile_b = carve(2 * TILES)
        step_t = carve(TILES)
        delta_t = carve(TILES)
        rows_f = carve(2 * TILES)
        sorted_f = carve(4)
        TILES_END = at[0]
        assert TILES_END <= NBLK * SB - RC * 7
        at[0] = SCATTERED = NBLK * SB - RC * 7
        slot_id = carve(RC, I32)
        meta = carve(RC * 6, I32)
        S = arena[:, :].rearrange("p (b w) -> p b w", b=NBLK)

        w_gnn = sb("w_gnn", 2 * 6 * D)
        rows = sb("rows", 940 + 3 * FT)
        X = sb("X", UNROLL * XS)
        PROH = sb("PROH", RING * (D + 1 + P))
        PR = PROH[:, 0:RING * (D + 1)]
        OH = PROH[:, RING * (D + 1):]
        stage = PROH[:, 0:SB]
        late = sb("late", 2)
        key_dst = sb("key_dst", 2)
        key_blk = sb("key_blk", UNROLL)
        outside = sb("outside", 2)
        away = sb("away", 2, I32)
        slot_to = sb("slot_to", UNROLL, I32)
        dist = sb("dist", 2 * P)
        first_e = sb("first_e", TILES)
        first_n = sb("first_n", TILES)
        iota_f = sb("iota_f", P)
        ident = sb("ident", P)
        before = sb("before", P)
        ones_m = sb("ones_m", P)
        small = sb("small", 18 * 2 * NBLK + 1)
        tile_blk_i = sb("tile_blk_i", 2 * TILES, I32, 1)
        last_row_i = sb("last_row_i", NBLK, I32, 1)
        tile_rows_i = sb("tile_rows_i", 2 * TILES, I32, 1)
        flag_i = sb("flag_i", 1, I32, 1)
        w_raw = X[:, 0:2 * 2 * 4 * D]
        Xv = X[:, :].rearrange("p (u w) -> p u w", u=UNROLL)
        Xi = X[:, :].bitcast(I32).rearrange("p (u w) -> p u w", u=UNROLL)
        PRv = PR.rearrange("p (u w) -> p u w", u=RING)
        OHv = OH.rearrange("p (u w) -> p u w", u=RING)

        def sm(i, cols=2 * NBLK, dt=F32):
            v = small[:, i * 2 * NBLK:i * 2 * NBLK + cols]
            return v if dt == F32 else v.bitcast(dt)

        eps_c = small[:, 18 * 2 * NBLK:]

        ST = X[:, 0:2 * 6 * P].rearrange("p (d k n) -> p d k n", d=2, k=6)
        free = X[:, 2 * 6 * P:]
        v_a, bf_r, bb_r, ga_r, be_r, xn_c, xT = (free[:, i * D:(i + 1) * D] for i in range(7))
        rb_r = rows[:, 0:NX]
        rwT = rows[:, NX:3 * NX]
        rw_raw = rows[0:NX, 3 * NX:3 * NX + D]
        lg = rows[:, 400:400 + NX]
        mx8 = rows[:, 440:448]
        mi8 = rows[:, 448:456].bitcast(mybir.dt.uint32)
        eid = rows[:, 460:460 + NBLK]
        valid = rows[:, 490:491]
        slot_x = rows[:, 500:500 + NBLK]
        slot_xi = rows[:, 530:530 + NBLK].bitcast(I32)
        ex = [rows[:, 560 + NX * i:560 + NX * (i + 1)] for i in range(8)]
        tile_e = rows[0:1, 820:820 + 2 * FT]
        tile_ei = rows[0:1, 940:940 + 3 * FT].bitcast(I32)
        M = w_gnn[:, 0:NX * NBLK]
        R1 = w_gnn[:, NX * NBLK:2 * NX * NBLK]
        R2 = w_gnn[:, 2 * NX * NBLK:3 * NX * NBLK]
        R3 = w_gnn[0:1, 0:FT * (NX - 1)]
        xt2, xT2, y2 = (X[:, i * ES * D:(i + 1) * ES * D].rearrange("p (s w) -> p s w", s=ES) for i in range(3))
        h2 = X[:, 12 * D:12 * D + ES * NH].rearrange("p (s w) -> p s w", s=ES)
        hT2 = X[:, 13 * D:13 * D + ES * P].rearrange("p (s w) -> p s w", s=ES)
        yg = xT2

        ps = [ctx.enter_context(nc.psum_tensor(f"ps{i}", [P, 1024], F32)) for i in range(4)]

        x_in, keys_in, next_in, w_in = sem("x_in"), sem("keys_in"), sem("next_in"), sem("w_in")
        const_ready = sem("const_ready")
        meta_id = sem("meta_id")
        v_step = sem("v_step")
        std_ready, var_ready = sem("std_ready"), sem("var_ready")
        h_ready, h_out = sem("h_ready"), sem("h_out")
        stats_done = sem("stats_done")
        init_out = sem("init_out")
        xs_init = sem("xs_init")
        cmp_done = [sem(f"cmp_done{d}") for d in range(2)]
        base_ready = sem("base_ready")
        scan_done = [sem(f"scan_done{d}") for d in range(2)]
        masked = [sem(f"masked{d}") for d in range(2)]
        pick_done = [sem(f"pick_done{d}") for d in range(2)]
        slots_ready = sem("slots_ready")
        meta_ready = sem("meta_ready")
        linear_out = sem("linear_out")
        last_known, from_init = sem("last_known"), sem("from_init")
        zeroed = sem("zeroed")
        to_out, tables_done, u_step = sem("to_out"), sem("tables_done"), sem("u_step")
        disorder_ready, disorder_sum = sem("disorder_ready"), sem("disorder_sum")
        tb_done, td_done, te_done = sem("tb_done"), sem("td_done"), sem("te_done")
        flag_ready = sem("flag_ready")
        wsum_ready, wt_ready, wt_read = sem("wsum_ready"), sem("wt_ready"), sem("wt_read")
        meta_in = [sem(f"meta_in{u}") for u in range(UNROLL)]
        late_done, key_dst_done, key_done = sem("late_done"), sem("key_dst_done"), sem("key_done")
        dist_ready, oh_ready = sem("dist_ready"), sem("oh_ready")
        edges_in = [sem(f"edges_in{u}") for u in range(UNROLL)]
        slot_known = [sem(f"slot_known{u}") for u in range(0, UNROLL, 2)]
        outside_done, away_done = sem("outside_done"), sem("away_done")
        got = [sem(f"got{u}") for u in range(UNROLL)]
        prod_ready = sem("prod_ready")
        sent = [sem(f"sent{u}") for u in range(UNROLL)]
        mm_done, summed = sem("mm_done"), sem("summed")
        loop_done = sem("loop_done")
        rows_in = sem("rows_in")
        staged, sT_ready, st_copied = sem("staged"), [sem(f"sT_ready{d}") for d in range(2)], [sem(f"st_copied{d}") for d in range(2)]
        agg_ready, agg_read, hx_in, xb_ready = sem("agg_ready"), sem("agg_read"), sem("hx_in"), sem("xb_ready")
        rwT_ready, rwT_copied = sem("rwT_ready"), sem("rwT_copied")
        block_done, x1_done, lg_done, mx_done = sem("block_done"), sem("x1_done"), sem("lg_done"), sem("mx_done")
        biased, leaky_done, res_done = sem("biased"), sem("leaky_done"), sem("res_done")
        r_sum, r_stat, r_std, r_rstd = sem("r_sum"), sem("r_stat"), sem("r_std"), sem("r_rstd")
        scaled, x1_sum, x1_stat, x1_std, x1_rstd = (
            sem(n) for n in ("scaled", "x1_sum", "x1_stat", "x1_std", "x1_rstd"))
        xn_staged, xT_ready, xT_copied, logits_ready = sem("xn_staged"), sem("xT_ready"), sem("xT_copied"), sem("logits_ready")
        picked, r_step = sem("picked"), sem("r_step")
        ffw_in = sem("ffw_in")
        onehot_ready, ranks_ready = sem("onehot_ready"), sem("ranks_ready")
        slots_x_ready, xs_out = sem("slots_x_ready"), sem("xs_out")
        xt_in = [sem(f"xt_in{s}") for s in range(ES)]
        f_xT, f_xTc, f_h, f_hc, f_hT, f_hTc, f_o, f_oc = (
            sem(n) for n in ("f_xT", "f_xTc", "f_h", "f_hc", "f_hT", "f_hTc", "f_o", "f_oc"))
        ys_out = [sem(f"ys_out{s}") for s in range(ES)]
        tiles_known = sem("tiles_known")
        ones_row = sem("ones_row")
        y_in = [sem(f"y_in{s}") for s in range(4)]
        out_ready = sem("out_ready")
        out_done = [sem(f"out_done{s}") for s in range(4)]

        f_h_ps = [ps[s][:, 512:512 + NH] for s in range(ES)]
        f_hT_ps = [ps[s][0:NH, 512 + NH:512 + NH + P] for s in range(ES)]
        f_o_ps = [ps[s][:, 512 + NH + P:512 + NH + P + D] for s in range(ES)]
        tot_ps = [ps[d][:, 0:NBLK] for d in range(2)]
        base_ps = [ps[d][:, 512:512 + NBLK] for d in range(2)]
        dis_ps = ps[2][:, 512:513]

        DEPTH = 6

        def has(i, lag):
            return not isinstance(i, int) or 0 <= i - lag < NBLK

        block = ctx.enter_context(nc.Block())

        @block.sync
        def _(sp):
            for i, k in ((FROM, src), (TO, dst)):
                sp.dma_start(keys[0:RP, i * RC:(i + 1) * RC],
                             k.rearrange("(p c) -> p c", c=RC)).then_inc(keys_in, 16)
            sp.wait_ge(const_ready, 13)
            xs = x_sb.rearrange("p (b d) -> p b d", b=NBLK)
            sp.dma_start(xs[:, 0:NBLK - 1, :],
                         x[0:(NBLK - 1) * P, :].rearrange("(b p) d -> p b d", p=P)).then_inc(x_in, 16)
            sp.dma_start(xs[0:TAIL, NBLK - 1, :], x[(NBLK - 1) * P:N, :]).then_inc(x_in, 16)
            sp.wait_ge(meta_id, 3)
            sp.dma_start(to_dram[0:SLOTS, :].rearrange("(p t) f -> p (t f)", p=P), to_init).then_inc(init_out, 16)
            last = (RP - 1) * RC
            sp.dma_start(next_i[0:RP - 1, :], dst[1:last + 1].rearrange("(p c) -> p c", c=RC)).then_inc(next_in, 16)
            sp.dma_start(next_i[RP - 1:RP, 0:RC - 1],
                         dst[last + 1:E].rearrange("(a c) -> a c", a=1)).then_inc(next_in, 16)
            wr = w_raw.rearrange("p (d o i) -> p d o i", d=2, o=2)
            for i, w in ((TO, w_fwd), (FROM, w_back)):
                sp.dma_start(wr[:, i], w.rearrange("(o p) i -> p o i", p=P)).then_inc(w_in, 16)
            sp.dma_start(from_dram[FULL * P:SLOTS, :].rearrange("(a p) w -> p a w", p=P),
                         empty.rearrange("p (a w) -> p a w", a=1).broadcast_to([P, TILES - FULL, SENT])).then_inc(from_init, 16)
            sp.wait_ge(last_known, 1)
            with sp.Fori(0, NBLK) as b:
                row = nc.values_load(last_row_i[0:1, bass.ds(b, 1)], engines=[mybir.EngineType.SP], min_val=0,
                                     max_val=SLOTS - P, skip_runtime_bounds_check_because="clamped when computed")
                sp.wait_ge(from_init, 16 * b + 16)
                sp.dma_start(from_dram[bass.ds(row, P), :], empty).then_inc(from_init, 16)
            sp.wait_ge(h_ready, 1)
            sp.dma_start(h_dram.rearrange("(b p) d -> p b d", p=P),
                         h_sb.rearrange("p (b d) -> p b d", b=NBLK)).then_inc(h_out, 16)
            sp.wait_ge(meta_ready, 1)
            sp.dma_start(to_dram[SLOTS:SLOTS + E, :].rearrange("(p c) f -> p (c f)", p=RP),
                         meta[0:RP, :]).then_inc(linear_out, 16)
            for c in range(D // P):
                sp.dma_start(xs_dram[:, c * P:(c + 1) * P].rearrange("(a p) w -> p a w", p=P),
                             ones_m[:, :].rearrange("p (a w) -> p a w", a=1).broadcast_to([P, FT, P])).then_inc(xs_init, 16)
            sp.wait_ge(tables_done, 1)
            sp.wait_ge(wt_read, 6)
            sp.wait_ge(flag_ready, 1)
            sp.wait_ge(linear_out, 16)

            def load_tiles(k, with_edges):
                assert 2 * UNROLL == 16
                k16 = 16 * k if isinstance(k, int) else sp.snap(16 * k)
                for h in range(0, UNROLL, 4):
                    _, row = nc.values_load_multi_w_load_instructions(
                        tile_rows_i[0:1, bass.ds(k16 + 2 * h, 8)], engines=[mybir.EngineType.SP],
                        min_val=0, max_val=SLOTS + E - P,
                        skip_runtime_bounds_check_because="clamped to the tables when computed")
                    for u in range(h, h + 4):
                        sp.wait_ge(mm_done, k * UNROLL + u + 1)
                        if not isinstance(k, int):
                            sp.wait_ge(sent[u], k16)
                        sp.dma_start(Xi[:, u, 2 * D:], to_dram[bass.ds(row[2 * (u - h) + 1], P), :]).then_inc(meta_in[u], 16)
                        if with_edges:
                            e0 = nc.s_assert_within(row[2 * (u - h)], 0, E - P, skip_runtime_bounds_check_because="clamped "
                                                    "to the edges when computed")
                            sp.dma_start(Xv[:, u, D:2 * D], edge[bass.ds(e0, P), :]).then_inc(edges_in[u], 16)

            sorted_reg = nc.values_load(flag_i[0:1, 0:1], engines=[mybir.EngineType.SP], min_val=0, max_val=1,
                                        skip_runtime_bounds_check_because="a comparison's 0 or 1")
            with sp.If(sorted_reg == 1):
                load_tiles(0, True)
                with sp.Fori(1, GROUPS) as k:
                    load_tiles(k, True)
            with sp.If(sorted_reg == 0):
                load_tiles(0, False)
                with sp.Fori(1, GROUPS) as k:
                    load_tiles(k, False)
            for u in range(UNROLL):
                sp.wait_ge(sent[u], 16 * GROUPS)
            with sp.Fori(GROUPS, 2 * GROUPS) as k:
                for u in range(UNROLL):
                    sp.wait_ge(mm_done, k * UNROLL + u + 1)
                    sp.dma_start(Xv[:, u, D:2 * D + 2],
                                 from_dram[bass.ds((k - GROUPS) * (UNROLL * P) + u * P, P), :]).then_inc(meta_in[u], 16)

            sp.wait_ge(loop_done, 1)
            for r, v in ((bf_r, b_fwd), (bb_r, b_back), (ga_r, gamma), (be_r, beta), (rb_r, router_b)):
                sp.dma_start(r, v.rearrange("(a n) -> a n", a=1).broadcast_to([P, v.shape[0]])).then_inc(rows_in, 16)
            sp.dma_start(rw_raw, router_w[:, :]).then_inc(rows_in, 16)

            def weights():
                sp.wait_ge(x1_done, NX // 2)
                w1_v = w1.rearrange("(c e) (k p) h -> p c e k h", e=2, p=P)
                w2_v = w2.rearrange("(c e) h n -> h c e n", e=2)
                b2_v = b2.rearrange("(a c e) n -> a c e n", a=1, e=2)
                b1_v = b1.rearrange("(a c e) n -> a c e n", a=1, e=2)
                for e in range(2):
                    at_e = W_AT + e * W_LEN
                    for k in range(2):
                        sp.dma_start(S[:, 0:NX // 2, at_e + k * NH:at_e + (k + 1) * NH],
                                     w1_v[:, :, e, k, :]).then_inc(ffw_in, 16)
                    sp.dma_start(S[0:NH, 0:NX // 2, at_e + 2 * NH:at_e + W_LEN], w2_v[:, :, e, :]).then_inc(ffw_in, 16)
                    sp.dma_start(S[NH:NH + 1, 0:NX // 2, at_e + 2 * NH:at_e + W_LEN],
                                 b2_v[:, :, e, :]).then_inc(ffw_in, 16)
                    sp.dma_start(S[0:1, 0:NX // 2, B1_AT + e * NH:B1_AT + (e + 1) * NH],
                                 b1_v[:, :, e, :]).then_inc(ffw_in, 16)

            def rows_of(b1_):
                b = b1_ - 1
                n = TAIL if isinstance(b, int) else P
                sp.wait_ge(xb_ready, b1_)
                sp.wait_ge(staged, b1_)
                sp.dma_start(arena[:, bass.ds(b * SB + D, D)], h_dram[bass.ds(b * P, P), :]).then_inc(hx_in, 16)
                sp.dma_start(arena[0:n, bass.ds(b * SB + 2 * D, D)], x[bass.ds(b * P, n), :]).then_inc(hx_in, 16)

            with sp.Fori(1, NX // 2 + 5) as b1_:
                rows_of(b1_)
            weights()
            with sp.Fori(NX // 2 + 5, NBLK) as b1_:
                rows_of(b1_)
            rows_of(NBLK)
            sp.wait_ge(xs_out, 16 * NBLK)
            with sp.Fori(0, FT // ES) as k:
                for s in range(ES):
                    sp.wait_ge(f_xT, ES * k + s + 1)
                    sp.dma_start(xt2[:, s, :], xs_dram[bass.ds((ES * k + s) * P, P), :]).then_inc(xt_in[s], 16)
            for b in range(NBLK):
                n = P if b < NBLK - 1 else TAIL
                sp.wait_ge(out_ready, b + 1)
                sp.dma_start(out[b * P:b * P + n, :], yg[0:n, b % 4, :]).then_inc(out_done[b % 4], 16)
            for s in range(4):
                sp.wait_ge(out_done[s], 16 * len(range(s, NBLK, 4)))

        @block.gpsimd
        def _(g):
            g.memset(x_sb.rearrange("p (b d) -> p b d", b=NBLK)[:, NBLK - 1, :], 0.0).then_inc(const_ready, 1)
            g.memset(next_i, 1 << 24).then_inc(const_ready, 1)
            g.iota(iota_f[:, :], pattern=[[1, P]], base=0, channel_multiplier=0,
                   allow_small_or_imprecise_dtypes=True).then_inc(const_ready, 1)
            g.iota(tile_n, pattern=[[1, TILES]], base=0, channel_multiplier=0,
                   allow_small_or_imprecise_dtypes=True).then_inc(const_ready, 1)
            g.memset(ident[:, :], 0.0).then_inc(const_ready, 1)
            g.memset(before[:, :], 1.0).then_inc(const_ready, 1)
            g.memset(ones_m[:, :], 1.0).then_inc(const_ready, 1)
            g.memset(ones_r, 1.0).then_inc(const_ready, 1)
            g.memset(PRv[:, :, D:D + 1], 1.0).then_inc(const_ready, 1)
            tv = to_init.rearrange("p (t f) -> p t f", f=6)
            tf = to_init.bitcast(F32).rearrange("p (t f) -> p t f", f=6)
            g.memset(to_init, 0).then_inc(const_ready, 1)
            g.memset(empty, 0.0).then_inc(const_ready, 1)
            g.wait_ge(const_ready, 11)
            g.memset(tf[:, :, KEY], NONE).then_inc(const_ready, 1)
            g.memset(tf[:, :, NDST], NONE).then_inc(meta_id, 1)
            g.iota(tv[:, :, SLOT], pattern=[[1, TILES]], base=0, channel_multiplier=TILES).then_inc(meta_id, 1)
            g.memset(empty[:, SENT - 1:SENT], NONE).then_inc(const_ready, 1)
            g.affine_select(out=ident[:, :], in_=ident[:, :], compare_op=ALU.not_equal, fill=1.0, base=0,
                            pattern=[[-1, P]], channel_multiplier=1).then_inc(const_ready, 1)
            g.affine_select(out=before[:, :], in_=before[:, :], compare_op=ALU.is_gt, fill=0.0, base=0,
                            pattern=[[1, P]], channel_multiplier=-1).then_inc(const_ready, 1)
            mt = meta.rearrange("p (c f) -> p c f", f=6)
            g.iota(mt[0:RP, :, EDGE], pattern=[[1, RC]], base=0, channel_multiplier=RC).then_inc(meta_id, 1)
            po = pos[0:RP, :]
            g.memset(po, 0.0).then_inc(pick_done[FROM], RANKS)
            with g.Fori(0, NBLK - RANKS + 1, RANKS) as b0:
                for j in range(RANKS):
                    g.wait_ge(masked[FROM], b0 + (j + 1))
                    g.wait_ge(pick_done[FROM], b0 + (j + RANKS))
                    g.tensor_tensor(po, po, rank[0:RP, j * RC:(j + 1) * RC], ALU.add).then_inc(pick_done[FROM], 1)
            g.memset(arena[:, TILES_END:SCATTERED], 0.0).then_inc(zeroed, 1)
            g.wait_ge(h_out, 16)
            g.memset(arena[:, 0:NODES_END], 0.0).then_inc(zeroed, 1)
            g.wait_ge(slots_ready, 1)
            g.wait_ge(init_out, 16)
            g.wait_ge(from_init, 16 * (NBLK + 1))
            g.memset(arena[:, NODES_END:EDGES_END], 0.0).then_inc(zeroed, 1)
            g.wait_ge(meta_id, 3)
            g.wait_ge(meta_ready, 1)
            g.wait_ge(flag_ready, 1)
            sorted_reg = nc.values_load(flag_i[0:1, 0:1], engines=[mybir.EngineType.Pool], min_val=0, max_val=1,
                                        skip_runtime_bounds_check_because="a comparison's 0 or 1")
            with g.If(sorted_reg == 0):
                for c in range(RC):
                    g.indirect_dma_start(
                        out=to_dram[:, :], out_offset=bass.IndirectOffsetOnAxis(ap=slot_id[0:RP, c:c + 1], axis=0),
                        in_=mt[0:RP, c, :], in_offset=None).then_inc(to_out, 16)
                g.wait_ge(to_out, 16 * RC)
            g.nop().then_inc(tables_done, 1)
            g.wait_ge(wt_read, 6)

            def gather(u, word, table_rows, at_, signal):
                g.indirect_dma_start(out=Xv[:, u, at_:at_ + D], out_offset=None, in_=table_rows[:, :],
                                     in_offset=bass.IndirectOffsetOnAxis(
                                         ap=Xi[:, u, 2 * D + word:2 * D + word + 1], axis=0)).then_inc(signal, 16)

            def send(u, loads):
                g.wait_ge(const_ready, 15)
                g.wait_ge(edges_in[u], loads)
                g.wait_ge(slot_known[u // 2], loads)
                g.indirect_dma_start(out=from_dram[:, :], out_offset=bass.IndirectOffsetOnAxis(
                    ap=slot_to[:, u:u + 1], axis=0),
                    in_=Xv[:, u, D:D + SENT], in_offset=None, bounds_check=SLOTS - 1, oob_is_err=False).then_inc(sent[u], 16)

            def first_pass(gather_edges):
                with g.Fori(16, 16 * GROUPS + 1, 16) as loads:
                    for u in range(UNROLL):
                        g.wait_ge(const_ready, 15)
                        g.wait_ge(meta_in[u], loads)
                        if gather_edges:
                            gather(u, EDGE, edge, D, edges_in[u])
                        gather(u, SRC, h_dram, 0, got[u])
                        if u >= 3:
                            send(u - 3, loads)
                    for u in range(UNROLL - 3, UNROLL):
                        send(u, loads)

            with g.If(sorted_reg == 1):
                first_pass(False)
            with g.If(sorted_reg == 0):
                first_pass(True)
            with g.Fori(16 * (GROUPS + 1), 16 * 2 * GROUPS + 1, 16) as loads:
                for u in range(UNROLL):
                    g.wait_ge(const_ready, 15)
                    g.wait_ge(meta_in[u], loads)
                    gather(u, DST, h_dram, 0, got[u])
            g.wait_ge(rows_in, 16 * 6)
            g.nop().then_inc(xb_ready, 1)
            with g.Fori(1, NBLK + 1) as b1_:
                b = b1_ - 1
                xb = arena[:, bass.ds(b * SB + 2 * D, D)]
                g.wait_ge(hx_in, 32 * b1_)
                g.tensor_tensor(xb, xb, be_r, ALU.add).then_inc(xb_ready, 1)
            g.wait_ge(xs_init, 16 * (D // P))
            g.wait_ge(slots_x_ready, 1)
            for b in range(NBLK):
                n = P if b < NBLK - 1 else TAIL
                g.indirect_dma_start(
                    out=xs_dram[:, :], out_offset=bass.IndirectOffsetOnAxis(ap=slot_xi[0:n, b:b + 1], axis=0),
                    in_=S[0:n, b, D:2 * D], in_offset=None).then_inc(xs_out, 16)
            for s in range(ES):
                g.wait_ge(ys_out[s], 16 * (FT // ES))
            for b in range(NBLK):
                n = P if b < NBLK - 1 else TAIL
                if b >= 4:
                    g.wait_ge(out_done[b % 4], 16 * (b // 4))
                g.indirect_dma_start(
                    out=yg[0:n, b % 4, :], out_offset=None, in_=ys_dram[:, :],
                    in_offset=bass.IndirectOffsetOnAxis(ap=slot_xi[0:n, b:b + 1], axis=0)).then_inc(y_in[b % 4], 16)

        @block.scalar
        def _(a):
            a.nop().then_inc(st_copied[0], 1)
            a.nop().then_inc(xT_copied, 1)
            a.wait_ge(var_ready, 1)
            a.activation(sm(1, NBLK), sm(0, NBLK), ACT.Sqrt).then_inc(std_ready, 1)
            for i in range(6):
                a.wait_ge(wt_ready, i + 1)
                a.activation(w_gnn[:, i * 2 * D:(i + 1) * 2 * D], ps[1 + i % 3][:, 0:2 * D], ACT.Copy).then_inc(wt_read, 1)
            a.wait_ge(flag_ready, 1)

            def one_hot(n, u, key):
                a.activation(dist[:, (u % 2) * P:(u % 2 + 1) * P], iota_f[:, :], ACT.Square, bias=key).then_inc(dist_ready, 1)
                a.wait_ge(mm_done, n + UNROLL - RING + 1)
                a.wait_ge(dist_ready, n + 1)
                a.activation(OHv[:, u % RING, :], dist[:, (u % 2) * P:(u % 2 + 1) * P], ACT.Relu, scale=-1.0,
                             bias=ones_m[:, 0:1]).then_inc(oh_ready, 1)

            with a.Fori(0, GROUPS) as k:
                for u in range(UNROLL):
                    n = k * UNROLL + u
                    w = u % 2
                    a.wait_ge(meta_in[u], 16 * k + 16)
                    a.activation(late[:, w:w + 1], Xi[:, u, 2 * D + EDGE:2 * D + EDGE + 1], ACT.Relu, scale=-1.0,
                                 bias=first_e[:, bass.ds(n, 1)]).then_inc(late_done, 1)
                    a.wait_ge(late_done, n + 1)
                    a.activation(key_dst[:, w:w + 1], late[:, w:w + 1], ACT.Identity, scale=4096.0,
                                 bias=Xv[:, u, 2 * D + NDST:2 * D + NDST + 1]).then_inc(key_dst_done, 1)
                    a.wait_ge(key_dst_done, n + 1)
                    a.activation(key_blk[:, u:u + 1], key_dst[:, w:w + 1], ACT.Identity,
                                 bias=first_n[:, bass.ds(n, 1)]).then_inc(key_done, 1)
                    a.wait_ge(key_done, n + 1)
                    one_hot(n, u, key_blk[:, u:u + 1])
            with a.Fori(GROUPS, 2 * GROUPS) as k:
                for u in range(UNROLL):
                    a.wait_ge(meta_in[u], 16 * k + 16)
                    one_hot(k * UNROLL + u, u, Xv[:, u, 2 * D + KEY:2 * D + KEY + 1])
            a.wait_ge(loop_done, 1)
            def turn(i):
                if has(i, 0):
                    b = i
                    a.wait_ge(sT_ready[1], b + 1)
                    a.activation(stage, arena[:, bass.ds(b * SB, SB)], ACT.Copy).then_inc(staged, 1)
                if has(i, 3):
                    b = i - 3
                    a.wait_ge(x1_stat, b + 1)
                    a.activation(sm(2, 1), sm(12, 2)[:, 1:2], ACT.Sqrt, bias=eps_c).then_inc(x1_std, 1)
                if has(i, 2):
                    b = i - 2
                    a.wait_ge(r_stat, b + 1)
                    a.activation(sm(0, 1), sm(13, 2)[:, 1:2], ACT.Sqrt, bias=eps_c).then_inc(r_std, 1)
                if has(i, 0):
                    b = i
                    a.wait_ge(sT_ready[0], b + 2)
                    a.activation(ST[:, 0], ps[0][:, 0:6 * P].rearrange("p (k n) -> p k n", k=6),
                                 ACT.Copy).then_inc(st_copied[0], 1)
                if has(i, 5):
                    b = i - 5
                    a.wait_ge(xT_ready, b + 2)
                    a.wait_ge(logits_ready, b + 1)
                    a.activation(xT, ps[2][:, 512:512 + 2 * P], ACT.Copy).then_inc(xT_copied, 1)
                if has(i, 4):
                    b = i - 4
                    a.wait_ge(block_done, b + 1)
                    a.wait_ge(xT_ready, b + 1)
                    a.activation(xn_c, arena[:, bass.ds(b * SB + D, D)], ACT.Copy).then_inc(xn_staged, 1)

            for i in range(DEPTH):
                turn(i)
            with a.Fori(DEPTH, NBLK) as i:
                turn(i)
            for i in range(NBLK, NBLK + DEPTH):
                turn(i)
            def rows_back(k):
                for s in range(ES):
                    a.wait_ge(f_xT, ES * (k + 1) + s + 1)
                    a.activation(xT2[:, s, :], ps[s][:, 0:2 * P], ACT.Copy).then_inc(f_xTc, 1)

            def hidden(k):
                for s in range(ES):
                    a.wait_ge(f_h, ES * k + s + 1)
                    a.activation(h2[:, s, :], f_h_ps[s], ACT.Relu).then_inc(f_hc, 1)

            def store(k):
                for s in range(ES):
                    a.wait_ge(f_oc, ES * (k + 1) + s + 1)
                    a.dma_start(ys_dram[bass.ds((ES * k + s) * P, P), :], y2[:, s, :]).then_inc(ys_out[s], 16)

            rows_back(0)
            hidden(0)
            with a.Fori(1, FT // ES) as k:
                rows_back(k)
                hidden(k)
                store(k - 1)
            store(FT // ES - 1)

        @block.vector
        def _(v):
            steps = [0]

            def done(ins):
                steps[0] += 1
                ins.then_inc(v_step, 1)
                v.wait_ge(v_step, steps[0])

            v.nop().then_inc(summed, RING)
            v.nop().then_inc(pick_done[TO], 1)
            v.nop().then_inc(st_copied[1], 1)
            v.nop().then_inc(agg_read, 1)
            v.nop().then_inc(picked, 1)
            v.nop().then_inc(f_oc, ES)
            done(v.memset(eps_c, EPS))
            v.wait_ge(const_ready, 15)
            mt = meta.rearrange("p (c f) -> p c f", f=6)
            tile_f, tend, off = sm(7), sm(14), sm(15)
            cnt = sm(4)

            def ranks_by_src():
                with v.Fori(0, NBLK - RANKS + 1, RANKS) as b0:
                    for j in range(RANKS):
                        b = b0 + j
                        v.wait_ge(pick_done[FROM], b + 1)
                        v.tensor_tensor_scan(rank[0:RP, j * RC:(j + 1) * RC], ones_r[0:RP, :],
                                             member[0:RP, bass.ds(b * RC, RC)], off[0:RP, bass.ds(b + FROM * NBLK, 1)],
                                             ALU.mult, ALU.add).then_inc(scan_done[FROM], 1)
                    for j in range(RANKS):
                        b = b0 + j
                        rk = rank[0:RP, j * RC:(j + 1) * RC]
                        v.wait_ge(scan_done[FROM], b + 1)
                        v.tensor_tensor(rk, rk, member[0:RP, bass.ds(b * RC, RC)], ALU.mult).then_inc(masked[FROM], 1)
                v.wait_ge(pick_done[FROM], NBLK + RANKS)

            def edge_slots(d, done):
                po = pos[0:RP, :]
                done(v.memset(po, 0.0))
                with v.Fori(1, NBLK + 1) as b1_:
                    b = b1_ - 1
                    mem = member[0:RP, bass.ds(b * RC, RC)]
                    rk = rank[0:RP, 0:RC]
                    v.wait_ge(pick_done[d], b1_)
                    v.tensor_tensor_scan(rk, ones_r[0:RP, :], mem, off[0:RP, bass.ds(b + d * NBLK, 1)],
                                         ALU.mult, ALU.add).then_inc(scan_done[d], 1)
                    v.wait_ge(scan_done[d], b1_)
                    v.tensor_tensor(rk, rk, mem, ALU.mult).then_inc(masked[d], 1)
                    v.wait_ge(masked[d], b1_)
                    v.tensor_tensor(po, po, rk, ALU.add).then_inc(pick_done[d], 1)
                v.wait_ge(pick_done[d], NBLK + 1)

            def normalise_and_sum_weights():
                v.wait_ge(x_in, 32)
                xs = x_sb.rearrange("p (b d) -> p b d", b=NBLK)
                hs = h_sb.rearrange("p (b d) -> p b d", b=NBLK)
                st6 = sm(10, 6 * NBLK)
                mv = sm(13, 2 * NBLK)
                for b in range(NBLK):
                    v.bn_stats(st6[:, 6 * b:6 * b + 6], xs[:, b, :]).then_inc(stats_done, 1)
                v.wait_ge(stats_done, NBLK)
                for b in range(NBLK):
                    v.bn_aggr(mv[:, 2 * b:2 * b + 2], st6[:, 6 * b:6 * b + 6]).then_inc(stats_done, 1)
                v.wait_ge(stats_done, 2 * NBLK)
                mv2 = mv.rearrange("p (b t) -> p b t", t=2)
                v.tensor_scalar(sm(0, NBLK), mv2[:, :, 1], EPS, None, ALU.add).then_inc(var_ready, 1)
                v.wait_ge(std_ready, 1)
                done(v.reciprocal(sm(0, NBLK), sm(1, NBLK)))
                for b in range(NBLK):
                    v.tensor_scalar(hs[:, b, :], xs[:, b, :], mv2[:, b, 0:1], sm(0, NBLK)[:, b:b + 1],
                                    ALU.subtract, ALU.mult).then_inc(stats_done, 1)
                v.wait_ge(stats_done, 3 * NBLK)
                v.nop().then_inc(h_ready, 1)
                v.wait_ge(w_in, 32)
                wr = w_raw.rearrange("p (d o i) -> p (d o) i", d=2, o=2)
                for part in range(2):
                    w = wr[:, :, part * D:(part + 1) * D]
                    v.tensor_tensor(w, w, wr[:, :, 2 * D:3 * D], ALU.add).then_inc(wsum_ready, 1)

            for d in (FROM, TO):
                kd, bi = (t[0:RP, d * RC:(d + 1) * RC] for t in (keys, blk_i))
                bh = blk_h[0:RP, d * (RC + 1):d * (RC + 1) + RC]
                v.wait_ge(keys_in, 32)
                done(v.tensor_scalar(bi, kd, 7, None, ALU.logical_shift_right))
                done(v.tensor_copy(bh, bi))
                with v.Fori(0, NBLK) as b:
                    v.tensor_scalar(member[0:RP, bass.ds(b * RC, RC)], bh,
                                    iota_f[0:RP, bass.ds(b, 1)], 0.0, ALU.is_equal, ALU.add,
                                    accum_out=cnt[0:RP, bass.ds(b + d * NBLK, 1)]).then_inc(cmp_done[d], 1)
                v.wait_ge(cmp_done[d], NBLK)
                if d == FROM:
                    done(v.tensor_scalar(low_i[0:RP, :], kd, P - 1, None, ALU.bitwise_and))
                    done(v.tensor_scalar(mt[0:RP, :, KEY].bitcast(F32), low_i[0:RP, :], -1.0, None, ALU.mult))
                    done(v.tensor_copy(mt[0:RP, :, SRC], kd))
                else:
                    done(v.tensor_scalar(mt[0:RP, :, NDST].bitcast(F32), kd, -1.0, None, ALU.mult))
                    done(v.tensor_copy(mt[0:RP, :, DST], kd))
                    v.nop().then_inc(meta_ready, 1)
                c25 = slice(d * NBLK, (d + 1) * NBLK)
                v.wait_ge(base_ready, 1 if d == FROM else 2)
                done(v.tensor_scalar(sm(5, dt=I32)[:, c25], tot_ps[d], float(P - 1), None, ALU.add))
                done(v.tensor_scalar(sm(6, dt=I32)[:, c25], sm(5, dt=I32)[:, c25], 7, None, ALU.logical_shift_right))
                done(v.tensor_copy(tile_f[:, c25], sm(6, dt=I32)[:, c25]))
                done(v.tensor_tensor_scan(tend[:, c25], ones_m[:, 0:NBLK], tile_f[:, c25], 0.0, ALU.mult, ALU.add))
                done(v.tensor_tensor(tile_f[:, c25], tend[:, c25], tile_f[:, c25], ALU.subtract))
                done(v.tensor_scalar(tile_f[:, c25], tile_f[:, c25], float(P), -1.0, ALU.mult, ALU.add))
                done(v.tensor_tensor(off[0:RP, c25], base_ps[d][0:RP, :], tile_f[0:RP, c25], ALU.add))
                if d == FROM:
                    done(v.tensor_scalar(sm(8, NBLK), tend[:, c25], float(P), -float(P), ALU.mult, ALU.add))
                    done(v.tensor_scalar(sm(8, NBLK), sm(8, NBLK), 0.0, None, ALU.max))
                    v.tensor_copy(last_row_i[:, :], sm(8, NBLK)[0:1, :]).then_inc(last_known, 1)
                if d == FROM:
                    ranks_by_src()
                    done(v.tensor_copy(mt[0:RP, :, SLOT], pos[0:RP, :]))
                    normalise_and_sum_weights()

            v.wait_ge(next_in, 32)
            nx = next_i[0:RP, :]
            done(v.tensor_scalar(row_i[0:RP, :], nx, 7, None, ALU.logical_shift_right))
            done(v.tensor_tensor(rank[0:RP, 0:RC], row_i[0:RP, :], blk_i[0:RP, TO * RC:(TO + 1) * RC], ALU.is_lt))
            v.tensor_reduce(sorted_f[0:RP, 0:1], rank[0:RP, 0:RC], AX.X, ALU.add).then_inc(disorder_ready, 1)
            v.wait_ge(disorder_sum, 1)
            done(v.tensor_scalar(sorted_f[:, 1:2], dis_ps, 0.0, None, ALU.is_equal))
            in_order = sorted_f[:, 1:2]
            done(v.tensor_copy(flag_i[0:1, :], in_order[0:1, :]))
            sorted_reg = nc.values_load(flag_i[0:1, 0:1], engines=[mybir.EngineType.DVE], min_val=0, max_val=1,
                                        skip_runtime_bounds_check_because="a comparison's 0 or 1")
            with v.If(sorted_reg == 0):
                u_steps = [0]

                def u_done(ins):
                    u_steps[0] += 1
                    ins.then_inc(u_step, 1)
                    v.wait_ge(u_step, u_steps[0])

                edge_slots(TO, u_done)
                u_done(v.tensor_copy(slot_id[0:RP, :], pos[0:RP, :]))
            v.nop().then_inc(slots_ready, 1)

            tbv = tile_b.rearrange("p (d t) -> p t d", d=2)
            done(v.memset(tile_b, 0.0))
            done(v.memset(delta_t, 0.0))
            done(v.tensor_tensor_scan(sm(8, NBLK), ones_m[:, 0:NBLK], tot_ps[TO], 0.0, ALU.mult, ALU.add))
            done(v.tensor_tensor(sm(8, NBLK), sm(8, NBLK), tot_ps[TO], ALU.subtract))
            done(v.tensor_tensor(sm(8, NBLK), sm(8, NBLK), tile_f[:, TO * NBLK:(TO + 1) * NBLK], ALU.subtract))
            done(v.tensor_tensor(sm(9, NBLK - 1), sm(8, NBLK)[:, 1:NBLK], sm(8, NBLK)[:, 0:NBLK - 1], ALU.subtract))
            v.nop().then_inc(tb_done, 1)
            v.nop().then_inc(td_done, 1)
            with v.Fori(1, NBLK) as b1_:
                b = b1_ - 1
                v.wait_ge(tb_done, b1_)
                v.scalar_tensor_tensor(tbv[:, :, FROM], tile_n, tend[:, bass.ds(b + FROM * NBLK, 1)],
                                       tbv[:, :, FROM], ALU.is_ge, ALU.add)
                v.wait_ge(td_done, b1_)
                v.tensor_scalar(step_t, tile_n, tend[:, bass.ds(b + TO * NBLK, 1)], sm(9, NBLK - 1)[:, bass.ds(b, 1)],
                                ALU.is_ge, ALU.mult).then_inc(te_done, 1)
                v.scalar_tensor_tensor(tbv[:, :, TO], tile_n, tend[:, bass.ds(b + TO * NBLK, 1)],
                                       tbv[:, :, TO], ALU.is_ge, ALU.add).then_inc(tb_done, 1)
                v.wait_ge(te_done, b1_)
                v.tensor_tensor(delta_t, delta_t, step_t, ALU.add).then_inc(td_done, 1)
            v.wait_ge(tb_done, NBLK)
            v.wait_ge(td_done, NBLK)
            done(v.tensor_copy(tile_blk_i[:, :], tile_b[0:1, :]))
            done(v.tensor_scalar(first_n[:, :], tbv[:, :, TO], float(P), None, ALU.mult))
            done(v.tensor_scalar(step_t, tile_n, float(P), -1.0, ALU.mult, ALU.add))
            done(v.tensor_scalar(delta_t, delta_t, sm(8, NBLK)[:, 0:1], None, ALU.add))
            done(v.tensor_tensor(delta_t, delta_t, step_t, ALU.add))
            done(v.tensor_scalar(first_e[:, :], delta_t, in_order, None, ALU.mult))
            rf = rows_f.rearrange("p (t f) -> p t f", f=2)
            done(v.tensor_scalar(rf[:, :, 0], delta_t, float(E - P), None, ALU.min))
            done(v.tensor_scalar(step_t, tile_n, float(P), None, ALU.mult))
            done(v.tensor_tensor(delta_t, rf[:, :, 0], step_t, ALU.subtract))
            done(v.tensor_scalar(delta_t, delta_t, float(SLOTS), in_order, ALU.add, ALU.mult))
            done(v.tensor_tensor(rf[:, :, 1], delta_t, step_t, ALU.add))
            done(v.tensor_copy(tile_rows_i[:, :], rows_f[0:1, :]))
            v.nop().then_inc(flag_ready, 1)

            done(v.memset(arena[:, EDGES_END:TILES_END], 0.0))
            v.wait_ge(tables_done, 1)
            v.wait_ge(linear_out, 16)
            done(v.memset(arena[:, SCATTERED:], 0.0))
            v.wait_ge(zeroed, 3)

            AHEAD = 2

            def product(d, k, u):
                if u >= UNROLL:
                    k, u = k + 1, u - UNROLL
                n = k * UNROLL + u
                if d == TO and u % 2 == 0:
                    pair = k * (UNROLL // 2) + u // 2
                    v.wait_ge(key_done, n + 2)
                    v.scalar_tensor_tensor(outside[:, :], key_blk[:, u:u + 2], P - 0.5, key_blk[:, u:u + 2],
                                           ALU.add, ALU.mult).then_inc(outside_done, 1)
                    v.wait_ge(outside_done, pair + 1)
                    v.tensor_scalar(away[:, :], outside[:, :], 0.0, float(1 << 20), ALU.is_gt,
                                    ALU.mult).then_inc(away_done, 1)
                    v.wait_ge(away_done, pair + 1)
                    v.tensor_tensor(slot_to[:, u:u + 2], away[:, :], Xi[:, u:u + 2, 2 * D + SLOT],
                                    ALU.add).then_inc(slot_known[u // 2], 16)
                v.wait_ge(mm_done, n + UNROLL - RING + 1)
                v.wait_ge(got[u], 16 * k + 16)
                if d == TO:
                    v.wait_ge(edges_in[u], 16 * k + 16)
                v.tensor_tensor(PRv[:, u % RING, 0:D], Xv[:, u, 0:D], Xv[:, u, D:2 * D],
                                ALU.mult).then_inc(prod_ready, 1)

            def sums_of(d, k, last):
                _, blocks = nc.values_load_multi_w_load_instructions(
                    tile_blk_i[0:1, bass.ds(k * UNROLL, UNROLL)], engines=[mybir.EngineType.DVE],
                    min_val=0, max_val=NBLK - 1,
                    skip_runtime_bounds_check_because="a count of at most NBLK - 1 comparisons that hold")
                for u in range(UNROLL):
                    if not last or u + AHEAD < UNROLL:
                        product(d, k, u + AHEAD)
                    sums = arena[:, bass.ds(blocks[u] * SB + d * SW, SW)]
                    n = k * UNROLL + u
                    v.wait_ge(mm_done, n + UNROLL + 1)
                    v.wait_ge(summed, n + RING)
                    v.tensor_tensor(sums, sums, ps[u % RING][:, 0:SW], ALU.add).then_inc(summed, 1)

            for d in (TO, FROM):
                for u in range(AHEAD):
                    product(d, d * GROUPS, u)
                with v.Fori(d * GROUPS, (d + 1) * GROUPS - 1) as k:
                    sums_of(d, k, False)
                sums_of(d, (d + 1) * GROUPS - 1, True)
            v.wait_ge(summed, 2 * TILES + RING)
            v.nop().then_inc(loop_done, 1)

            v.wait_ge(rows_in, 16 * 6)
            v.wait_ge(rwT_ready, 1)
            done(v.tensor_copy(rwT, ps[3][:, 512:512 + 2 * NX]))
            v.nop().then_inc(rwT_copied, 1)
            rinv = sm(1, NBLK)
            done(v.tensor_tensor(rinv, S[:, :, SW - 1], S[:, :, 2 * SW - 1], ALU.add))
            done(v.tensor_scalar(rinv, rinv, 1.0, None, ALU.max))
            done(v.reciprocal(rinv, rinv))

            def col(t, c, n=1):
                return t[:, bass.ds(c, n)]

            def turn(i):
                if has(i, 6):
                    b = i - 6
                    b1_ = b + 1 if isinstance(b, int) else v.snap(b + 1)
                    v.wait_ge(picked, b1_)
                    v.wait_ge(logits_ready, b1_ + 1)
                    v.tensor_tensor(lg, ps[3][:, 0:NX], rb_r, ALU.add).then_inc(lg_done, 1)
                    v.wait_ge(const_ready, 15)
                    v.wait_ge(lg_done, b1_)
                    v.max(mx8, lg).then_inc(mx_done, 1)
                    v.wait_ge(const_ready, 15)
                    v.wait_ge(mx_done, b1_)
                    v.max_index(mi8, mx8, lg).then_inc(r_step, 1)
                    v.wait_ge(r_step, b1_)
                    v.tensor_copy(col(eid, b), mi8[:, 0:1]).then_inc(picked, 1)
                if has(i, 1):
                    b = i - 1
                    v.wait_ge(agg_ready, b + 1)
                    v.scalar_tensor_tensor(v_a, bf_r, col(arena, b * SB + SW - 1), ps[2][:, 0:D],
                                           ALU.mult, ALU.add).then_inc(agg_read, 1)
                if has(i, 0):
                    v.wait_ge(sT_ready[1], i + 2)
                    v.tensor_copy(ST[:, 1], ps[1][:, 0:6 * P].rearrange("p (k n) -> p k n", k=6)).then_inc(st_copied[1], 1)
                if has(i, 3):
                    b = i - 3
                    b1_ = b + 1 if isinstance(b, int) else v.snap(b + 1)
                    v.wait_ge(x1_std, b1_)
                    v.reciprocal(sm(17, 1), sm(2, 1)).then_inc(x1_rstd, 1)
                    v.wait_ge(x1_rstd, b1_)
                    v.tensor_scalar(col(arena, b * SB + D, D), col(arena, b * SB, D), sm(12, 1), sm(17, 1),
                                    ALU.subtract, ALU.mult).then_inc(block_done, 1)
                if has(i, 2):
                    b = i - 2
                    b1_ = b + 1 if isinstance(b, int) else v.snap(b + 1)
                    x1 = col(arena, b * SB, D)
                    v.wait_ge(r_std, b1_)
                    v.reciprocal(sm(16, 1), sm(0, 1)).then_inc(r_rstd, 1)
                    v.scalar_tensor_tensor(x1, x1, sm(13, 1), ga_r, ALU.subtract, ALU.mult).then_inc(scaled, 1)
                    v.wait_ge(r_rstd, b1_)
                    v.wait_ge(scaled, b1_)
                    v.scalar_tensor_tensor(x1, x1, sm(16, 1), col(arena, b * SB + 2 * D, D),
                                           ALU.mult, ALU.add).then_inc(x1_done, 1)
                    v.wait_ge(const_ready, 15)
                    v.wait_ge(x1_done, b1_)
                    v.bn_stats(sm(11, 6), x1).then_inc(x1_sum, 1)
                    v.wait_ge(const_ready, 15)
                    v.wait_ge(x1_sum, b1_)
                    v.bn_aggr(sm(12, 2), sm(11, 6)).then_inc(x1_stat, 1)
                if has(i, 1):
                    b = i - 1
                    b1_ = b + 1 if isinstance(b, int) else v.snap(b + 1)
                    at_b = b * SB if isinstance(b, int) else v.snap(b * SB)
                    r = col(arena, at_b, D)
                    v.wait_ge(agg_read, b + 2)
                    v.scalar_tensor_tensor(v_a, bb_r, col(arena, at_b + 2 * SW - 1), v_a,
                                           ALU.mult, ALU.add).then_inc(biased, 1)
                    v.wait_ge(biased, b1_)
                    v.scalar_tensor_tensor(v_a, v_a, SLOPE, v_a, ALU.mult, ALU.max).then_inc(leaky_done, 1)
                    v.wait_ge(xb_ready, b + 2)
                    v.wait_ge(leaky_done, b1_)
                    v.scalar_tensor_tensor(r, v_a, col(rinv, b), col(arena, at_b + D, D),
                                           ALU.mult, ALU.add).then_inc(res_done, 1)
                    v.wait_ge(const_ready, 15)
                    v.wait_ge(res_done, b1_)
                    v.bn_stats(sm(10, 6), r).then_inc(r_sum, 1)
                    v.wait_ge(const_ready, 15)
                    v.wait_ge(r_sum, b1_)
                    v.bn_aggr(sm(13, 2), sm(10, 6)).then_inc(r_stat, 1)

            for i in range(DEPTH):
                turn(i)
            with v.Fori(DEPTH, NBLK) as i:
                turn(i)
            for i in range(NBLK, NBLK + DEPTH + 1):
                turn(i)
            v.wait_ge(picked, NBLK + 1)

            Mv = M.rearrange("p (e b) -> p e b", e=NX)
            ib = iota_f[:, 0:NX].rearrange("p (e a) -> p e a", a=1).broadcast_to([P, NX, NBLK])
            eb = eid.rearrange("p (a b) -> p a b", a=1).broadcast_to([P, NX, NBLK])
            done(v.tensor_tensor(Mv, ib, eb, ALU.is_equal))
            done(v.tensor_reduce(valid, ident[:, 0:TAIL], AX.X, ALU.add))
            done(v.tensor_scalar(Mv[:, :, NBLK - 1], Mv[:, :, NBLK - 1], valid, None, ALU.mult))
            v.nop().then_inc(onehot_ready, 1)
            v.wait_ge(ranks_ready, 1)
            half = NX * NBLK // 2
            rk_ps = [ps[0][:, 0:half], ps[0][:, 512:512 + half]]
            ct_ps = [ps[1][:, 0:half], ps[1][:, 512:512 + half]]
            for i in range(2):
                done(v.tensor_copy(R1[:, i * half:(i + 1) * half], ct_ps[i]))
            one = ones_m[:, 0:1].broadcast_to([P, NX * NBLK])
            done(v.tensor_tensor_scan(R2, one, R1, 0.0, ALU.mult, ALU.add))
            ex_c, ex_i, ex_t, ex_e, ex_s, ex_p = ex[0], ex[1].bitcast(I32), ex[2], ex[3], ex[4], ex[5]
            done(v.tensor_reduce(ex_c, R1.rearrange("p (e b) -> p e b", e=NX), AX.X, ALU.add))
            done(v.tensor_scalar(ex_i, ex_c, float(P - 1), None, ALU.add))
            done(v.tensor_scalar(ex_s.bitcast(I32), ex_i, 7, None, ALU.logical_shift_right))
            done(v.tensor_copy(ex_t, ex_s.bitcast(I32)))
            done(v.tensor_tensor_scan(ex_e, ones_m[:, 0:NX], ex_t, 0.0, ALU.mult, ALU.add))
            done(v.tensor_tensor(ex_t, ex_e, ex_t, ALU.subtract))
            done(v.tensor_tensor_scan(ex_s, ones_m[:, 0:NX], ex_c, 0.0, ALU.mult, ALU.add))
            done(v.tensor_tensor(ex_s, ex_s, ex_c, ALU.subtract))
            done(v.scalar_tensor_tensor(ex_p, ex_t, float(P), ex_s, ALU.mult, ALU.subtract))
            done(v.tensor_tensor(R2, R2, R1, ALU.subtract))
            for i in range(2):
                part = R2[:, i * half:(i + 1) * half]
                done(v.tensor_tensor(part, part, rk_ps[i], ALU.add))
            R2v = R2.rearrange("p (e b) -> p e b", e=NX)
            done(v.tensor_tensor(R2v, R2v, ex_p.rearrange("p (e a) -> p e a", a=1).broadcast_to([P, NX, NBLK]), ALU.add))
            done(v.tensor_tensor(R2, R2, M, ALU.mult))
            done(v.tensor_reduce(slot_x, R2.rearrange("p (e b) -> p b e", e=NX), AX.X, ALU.add))
            done(v.tensor_copy(slot_xi, slot_x))
            v.nop().then_inc(slots_x_ready, 1)
            tv = R3.rearrange("p (t e) -> p t e", e=NX - 1)
            done(v.tensor_tensor(tv, iota_f[0:1, 0:FT].rearrange("p (t a) -> p t a", a=1).broadcast_to([1, FT, NX - 1]),
                                 ex_e[0:1, 0:NX - 1].rearrange("p (a e) -> p a e", a=1).broadcast_to([1, FT, NX - 1]),
                                 ALU.is_ge))
            te = tile_e[:, 0:FT]
            done(v.tensor_reduce(te, tv, AX.X, ALU.add))
            ti = tile_ei.rearrange("p (f t) -> p f t", f=3)
            done(v.tensor_copy(ti[:, 0, :], te))
            done(v.tensor_scalar(ti[:, 1, :], ti[:, 0, :], 1, None, ALU.logical_shift_right))
            done(v.tensor_scalar(ti[:, 2, :], ti[:, 0, :], 1, None, ALU.bitwise_and))
            done(v.tensor_scalar(te, ti[:, 1, :], float(SB), None, ALU.mult))
            tp = ti.rearrange("p f t -> p (f t)")[:, 0:2 * FT].rearrange("p (t f) -> p t f", f=2)
            ww = tile_e.rearrange("p (f t) -> p f t", f=2)[:, 1, :]
            done(v.scalar_tensor_tensor(ww, ti[:, 2, :], float(W_LEN), te, ALU.mult, ALU.add))
            done(v.scalar_tensor_tensor(te, ti[:, 2, :], float(NH), te, ALU.mult, ALU.add))
            done(v.tensor_copy(tp[:, :, 0], ww))
            done(v.tensor_copy(tp[:, :, 1], te))
            v.nop().then_inc(tiles_known, 1)

            done(v.memset(hT2[NH:NH + 1, :, :], 1.0))
            v.nop().then_inc(ones_row, 1)

            def expert_tiles(k):
                for s in range(ES):
                    v.wait_ge(f_hT, ES * k + s + 1)
                    v.tensor_copy(hT2[0:NH, s, :], f_hT_ps[s]).then_inc(f_hTc, 1)
                for s in range(ES):
                    v.wait_ge(f_o, ES * k + s + 1)
                    if not isinstance(k, int):
                        v.wait_ge(ys_out[s], 16 * k)
                    v.tensor_scalar(y2[:, s, :], f_o_ps[s], 0.0, None, ALU.max).then_inc(f_oc, 1)

            expert_tiles(0)
            with v.Fori(1, FT // ES) as k:
                expert_tiles(k)
            for b in range(NBLK):
                n = P if b < NBLK - 1 else TAIL
                v.wait_ge(y_in[b % 4], 16 * (b // 4 + 1))
                y = yg[0:n, b % 4, :]
                v.tensor_tensor(y, y, S[0:n, b, 0:D], ALU.add).then_inc(out_ready, 1)

        @block.tensor
        def _(pe):
            pe.nop().then_inc(mm_done, UNROLL)
            pe.nop().then_inc(sT_ready[0], 1)
            pe.nop().then_inc(sT_ready[1], 1)
            pe.nop().then_inc(logits_ready, 1)
            pe.nop().then_inc(xT_ready, 1)
            pe.nop().then_inc(f_xT, ES)
            cnt = sm(4)
            pe.wait_ge(const_ready, 15)
            for d in (FROM, TO):
                pe.wait_ge(cmp_done[d], NBLK)
                nc.tensor.matmul(tot_ps[d], ones_m[0:RP, :], cnt[0:RP, d * NBLK:(d + 1) * NBLK], start=True, stop=True)
                nc.tensor.matmul(base_ps[d], before[0:RP, :], cnt[0:RP, d * NBLK:(d + 1) * NBLK],
                                 start=True, stop=True).then_inc(base_ready, 1)
            pe.wait_ge(disorder_ready, 1)
            nc.tensor.matmul(dis_ps, ones_m[0:RP, :], sorted_f[0:RP, 0:1], start=True, stop=True).then_inc(disorder_sum, 1)
            pe.wait_ge(wsum_ready, 2)
            pe.wait_ge(flag_ready, 1)
            ws = w_raw.rearrange("p (d o i) -> p d o i", d=2, o=2)
            for i in range(6):
                if i >= 3:
                    pe.wait_ge(wt_read, i - 2)
                for j in range(2):
                    d, kk = (2 * i + j) // 6, (2 * i + j) % 6
                    col = kk * P if kk < 4 else (kk + 2) * P
                    for o in range(2):
                        last = nc.tensor.transpose(ps[1 + i % 3][:, (2 * j + o) * P:(2 * j + o + 1) * P],
                                                   ws[:, d, o, col:col + P], ident[:, :])
                last.then_inc(wt_ready, 1)
            pe.wait_ge(wt_read, 6)
            with pe.Fori(0, 2 * GROUPS) as k:
                for u in range(UNROLL):
                    n = k * UNROLL + u
                    pe.wait_ge(prod_ready, n + 1)
                    pe.wait_ge(oh_ready, n + 1)
                    pe.wait_ge(summed, n + 1)
                    acc = ps[u % RING]
                    nc.tensor.matmul(acc[:, 0:512], OHv[:, u % RING, :], Xv[:, u, 0:2 * D], start=True, stop=True)
                    nc.tensor.matmul(acc[:, 512:SW], OHv[:, u % RING, :], PRv[:, u % RING, :], start=True,
                                     stop=True).then_inc(mm_done, 1)
            pe.wait_ge(loop_done, 1)
            pe.wait_ge(rows_in, 16 * 6)
            for kk in range(2):
                last = nc.tensor.transpose(ps[3][:, 512 + kk * NX:512 + (kk + 1) * NX],
                                           rw_raw[:, kk * P:(kk + 1) * P], ident[0:NX, 0:NX])
            last.then_inc(rwT_ready, 1)
            pe.wait_ge(rwT_copied, 1)
            def transposes(d, b):
                pe.wait_ge(st_copied[d], b + 1)
                for kk in range(6):
                    last = nc.tensor.transpose(ps[d][:, kk * P:(kk + 1) * P],
                                               stage[:, d * SW + kk * P:d * SW + (kk + 1) * P], ident[:, :])
                last.then_inc(sT_ready[d], 1)

            def products(d, b):
                pe.wait_ge(st_copied[d], b + 2)
                for kk in range(6):
                    last = nc.tensor.matmul(ps[2][:, 0:D], ST[:, d, kk, :],
                                            w_gnn[:, (d * 6 + kk) * D:(d * 6 + kk + 1) * D],
                                            start=(d == 0 and kk == 0), stop=(d == 1 and kk == 5))
                return last

            def turn(i):
                if has(i, 1):
                    pe.wait_ge(agg_read, i)
                    products(0, i - 1)
                if has(i, 0):
                    pe.wait_ge(staged, i + 1)
                    transposes(0, i)
                if has(i, 1):
                    products(1, i - 1).then_inc(agg_ready, 1)
                if has(i, 0):
                    transposes(1, i)
                if has(i, 4):
                    b = i - 4
                    pe.wait_ge(xn_staged, b + 1)
                    pe.wait_ge(xT_copied, b + 1)
                    for kk in range(2):
                        last = nc.tensor.transpose(ps[2][:, 512 + kk * P:512 + (kk + 1) * P],
                                                   xn_c[:, kk * P:(kk + 1) * P], ident[:, :])
                    last.then_inc(xT_ready, 1)
                if has(i, 5):
                    b = i - 5
                    pe.wait_ge(xT_copied, b + 2)
                    pe.wait_ge(picked, b + 1)
                    for kk in range(2):
                        last = nc.tensor.matmul(ps[3][:, 0:NX], xT[:, kk * P:(kk + 1) * P],
                                                rwT[:, kk * NX:(kk + 1) * NX], start=(kk == 0), stop=(kk == 1))
                    last.then_inc(logits_ready, 1)

            for i in range(DEPTH):
                turn(i)
            with pe.Fori(DEPTH, NBLK) as i:
                turn(i)
            for i in range(NBLK, NBLK + DEPTH):
                turn(i)
            pe.wait_ge(onehot_ready, 1)
            half = NX * NBLK // 2
            for i in range(2):
                nc.tensor.matmul(ps[0][:, i * 512:i * 512 + half], before[:, :], M[:, i * half:(i + 1) * half],
                                 start=True, stop=True)
                last = nc.tensor.matmul(ps[1][:, i * 512:i * 512 + half], ones_m[:, :], M[:, i * half:(i + 1) * half],
                                        start=True, stop=True)
            last.then_inc(ranks_ready, 1)
            pe.wait_ge(tiles_known, 1)
            pe.wait_ge(ones_row, 1)
            pe.wait_ge(ffw_in, 16 * 10)

            def rows_T(k):
                for s in range(ES):
                    pe.wait_ge(xt_in[s], 16 * k + 16)
                    for kk in range(2):
                        last = nc.tensor.transpose(ps[s][:, kk * P:(kk + 1) * P],
                                                   xt2[:, s, kk * P:(kk + 1) * P], ident[:, :])
                    last.then_inc(f_xT, 1)

            def layers(k, more):
                _, at_ = nc.values_load_multi_w_load_instructions(
                    tile_ei[0:1, bass.ds(k * 2 * ES, 2 * ES)], engines=[mybir.EngineType.PE],
                    min_val=0, max_val=(NX // 2 - 1) * SB + W_LEN,
                    skip_runtime_bounds_check_because="a count of at most NX - 1 comparisons, scaled")
                for s in range(ES):
                    pe.wait_ge(f_xTc, ES * k + s + 1)
                    pe.wait_ge(f_oc, ES * k + s + 1)
                    h = f_h_ps[s]
                    nc.tensor.matmul(h, ones_m[0:1, :], arena[0:1, bass.ds(at_[2 * s + 1] + B1_AT, NH)],
                                     start=True, stop=False)
                    for kk in range(2):
                        last = nc.tensor.matmul(h, xT2[:, s, kk * P:(kk + 1) * P],
                                                arena[:, bass.ds(at_[2 * s] + W_AT + kk * NH, NH)],
                                                start=False, stop=(kk == 1))
                    last.then_inc(f_h, 1)
                for s in range(ES):
                    copied = ES * k + s + 1 if isinstance(k, int) else pe.snap(ES * k + s + 1)
                    pe.wait_ge(const_ready, 15)
                    pe.wait_ge(f_hc, copied)
                    nc.tensor.transpose(f_hT_ps[s], h2[:, s, :], ident[:, :]).then_inc(f_hT, 1)
                if more:
                    rows_T(k + 1)
                for s in range(ES):
                    pe.wait_ge(f_hTc, ES * k + s + 1)
                    nc.tensor.matmul(f_o_ps[s], hT2[0:NH + 1, s, :],
                                     arena[0:NH + 1, bass.ds(at_[2 * s] + W_AT + 2 * NH, D)],
                                     start=True, stop=True).then_inc(f_o, 1)

            rows_T(0)
            with pe.Fori(0, FT // ES - 1) as k:
                layers(k, True)
            layers(FT // ES - 1, False)


_INS = ['x', 'src', 'dst', 'edge_attr_256', 'L0_gnn_W_fwd', 'L0_gnn_b_fwd', 'L0_gnn_W_back', 'L0_gnn_b_back',
        'L0_gnn_gamma', 'L0_gnn_beta', 'L0_ffn_router_w', 'L0_ffn_router_b', 'L0_ffn_W1', 'L0_ffn_b1',
        'L0_ffn_W2', 'L0_ffn_b2']


def kernel(**inputs):
    import numpy as _np
    import concourse.bacc as _bacc
    from concourse import mybir as _mybir
    from concourse.bass_utils import run_bass_kernel_spmd as _run

    nc = _bacc.Bacc("TRN2", target_bir_lowering=False, num_devices=1)
    arrays, args = {}, []
    for name in _INS:
        a = _np.ascontiguousarray(inputs[name])
        arrays[f"in_{name}_dram"] = a
        args.append(nc.dram_tensor(f"in_{name}_dram", a.shape, _mybir.dt.from_np(a.dtype), kind="ExternalInput").ap())
    out = nc.dram_tensor("out_0_dram", (N, D), _mybir.dt.float32, kind="ExternalOutput").ap()
    gnn_ffn(nc, *args, out)
    r = _run(nc, [arrays], core_ids=[0])
    return r.results[0]["out_0_dram"]
```
